# Optimizing a Trainium2 kernel written in Bass

```python
import numpy as np
import jax
import jax.numpy as jnp

def _softmax(x, axis=-1):
    return jax.nn.softmax(x, axis=axis)

def _gelu(x):
    return jax.nn.gelu(x, approximate=True)

def _silu(x):
    return jax.nn.silu(x)

def _sigmoid(x):
    return jax.nn.sigmoid(x)

def _layernorm(x, axis=-1, eps=1e-05):
    m = jnp.mean(x, axis=axis, keepdims=True)
    v = jnp.var(x, axis=axis, keepdims=True)
    return (x - m) / jnp.sqrt(v + eps)

def _scatter_add(tgt, idx, src, axis=0):
    return tgt.at[idx].add(src)

def _segment_sum(src, seg, n):
    return jax.ops.segment_sum(src, seg, n)
kernel_name = 'mk_flamingo_gated_d1_seqx_r8_bb7a4f'

def setup_inputs(seed: int=0):
    np.random.seed(seed)
    _w = jnp.asarray

    def _rec_inputs():
        import jax
        import jax.numpy as jnp
        _rk = jax.random.key(seed)
        x = 0.000341 + 1 * jax.random.normal(jax.random.fold_in(_rk, 1), (16, 128, 256), jnp.float32)
        _lenS = 128 - jax.random.randint(jax.random.fold_in(_rk, 7), (16,), 0, max(1, 128 // 4) + 1, jnp.int32)
        _lenS2 = 128 - jax.random.randint(jax.random.fold_in(_rk, 8), (16,), 0, max(1, 128 // 4) + 1, jnp.int32)
        _ctx_2048P = jax.random.normal(jax.random.fold_in(_rk, 11), (16, 16, 256), jnp.float32)
        _ctx_2048c = jax.random.dirichlet(jax.random.fold_in(_rk, 511), 0.3 * jnp.ones((16,), jnp.float32), (16, 128))
        _ctx_2048t = jnp.einsum('bsk,bkd->bsd', _ctx_2048c, _ctx_2048P)
        _ctx_2048t = _ctx_2048t * jax.lax.rsqrt(jnp.mean(jnp.square(_ctx_2048t)) + 1e-12) * 0.953939
        ctx_2048 = -1.47943e-05 + 1.00017 * (_ctx_2048t + 0.3 * jax.random.normal(jax.random.fold_in(_rk, 611), (16, 128, 256), jnp.float32))
        _g = jax.random.normal(jax.random.fold_in(_rk, 9001), (2, 1), jnp.float32)
        _g = jnp.sign(_g) * jnp.maximum(jnp.abs(_g), 1.0) + (_g == 0) * 1.0
        g_xattn = _g[0]
        g_ffn = _g[1]
        return (x, ctx_2048, g_xattn, g_ffn)
    x, ctx_2048, g_xattn, g_ffn = _rec_inputs()

    def _L0_xattn_setup():
        import jax, jax.numpy as jnp
        import numpy as np

        def _wkv(time_decay, time_first, k, v):
            w = -jnp.exp(time_decay)
            u = time_first
            B, T, C = k.shape
            aa = jnp.zeros((B, C), dtype=k.dtype)
            bb = jnp.zeros((B, C), dtype=k.dtype)
            pp = jnp.full((B, C), -1e+38, dtype=k.dtype)

            def step(carry, kv_t):
                aa, bb, pp = carry
                kt, vt = kv_t
                ww = u + kt
                q = jnp.maximum(pp, ww)
                e1 = jnp.exp(pp - q)
                e2 = jnp.exp(ww - q)
                y_t = (e1 * aa + e2 * vt) / (e1 * bb + e2)
                ww2 = pp + w
                q2 = jnp.maximum(ww2, kt)
                e1b = jnp.exp(ww2 - q2)
                e2b = jnp.exp(kt - q2)
                new_carry = (e1b * aa + e2b * vt, e1b * bb + e2b, q2)
                return (new_carry, y_t)
            ks = jnp.transpose(k, (1, 0, 2))
            vs = jnp.transpose(v, (1, 0, 2))
            _, ys = jax.lax.scan(step, (aa, bb, pp), (ks, vs))
            return jnp.transpose(ys, (1, 0, 2))
        key = jax.random.key(seed)
        k1, k2, k3, k4 = jax.random.split(key, 4)
        B, T, C = (8, 128, 256)
        return {'batch_size': B, 'seq_len': T, 'embedding_dim': C, 'time_decay': jax.random.normal(k1, (C,), dtype=jnp.float32), 'time_first': jax.random.normal(k2, (C,), dtype=jnp.float32), 'k': jax.random.normal(k3, (B, T, C), dtype=jnp.float32), 'v': jax.random.normal(k4, (B, T, C), dtype=jnp.float32)}
    _L0_xattn_all = _L0_xattn_setup()
    _L0_xattn_in = {k: v for k, v in _L0_xattn_all.items() if k in ('time_decay', 'time_first')}
    del _L0_xattn_all

    def _L0_ffn_setup():
        import jax, jax.numpy as jnp
        import numpy as np
        B, S, D = (2, 256, 256)
        MOE_D = 176
        E = 16
        K = 6
        ALPHA = 0.001

        def _moe_forward(x, gate_w, w_gate, w_up, w_down):
            b, s, d = x.shape
            T = b * s
            h = x.reshape(T, d)
            logits = h @ gate_w.T
            scores = jax.nn.softmax(logits.astype(jnp.float32), axis=-1)
            topk_w, topk_idx = jax.lax.top_k(scores, K)
            cw = jnp.zeros((T, E), jnp.float32)
            cw = cw.at[jnp.arange(T)[:, None], topk_idx].add(topk_w)
            y = jnp.zeros((T, d), x.dtype)
            for e in range(E):
                g = h @ w_gate[e].T
                u = h @ w_up[e].T
                out = jax.nn.silu(g) * u @ w_down[e].T
                y = y + cw[:, e:e + 1].astype(x.dtype) * out
            counts = jnp.sum(jax.nn.one_hot(topk_idx.reshape(b, s * K), E, dtype=jnp.float32), axis=1)
            ce = counts * (E / (s * K))
            scores_bse = scores.reshape(b, s, E)
            aux = jnp.mean(jnp.sum(ce * scores_bse.mean(axis=1), axis=1)) * ALPHA
            return (y.reshape(b, s, d), aux)
        key = jax.random.key(seed)
        ks = jax.random.split(key, 5)
        sd = 1.0 / np.sqrt(D)
        sm = 1.0 / np.sqrt(MOE_D)
        return {'x': jax.random.normal(ks[0], (B, S, D), jnp.float32), 'gate_w': jax.random.normal(ks[1], (E, D), jnp.float32) * sd, 'w_gate': jax.random.normal(ks[2], (E, MOE_D, D), jnp.float32) * sd, 'w_up': jax.random.normal(ks[3], (E, MOE_D, D), jnp.float32) * sd, 'w_down': jax.random.normal(ks[4], (E, D, MOE_D), jnp.float32) * sm}
    _L0_ffn_all = _L0_ffn_setup()
    _L0_ffn_in = {k: v for k, v in _L0_ffn_all.items() if k in ('gate_w', 'w_gate', 'w_up', 'w_down')}
    del _L0_ffn_all
    return {'x': x, 'ctx_2048': ctx_2048, 'g_xattn': g_xattn, 'g_ffn': g_ffn, 'L0_xattn_time_decay': _L0_xattn_in['time_decay'], 'L0_xattn_time_first': _L0_xattn_in['time_first'], 'L0_ffn_gate_w': _L0_ffn_in['gate_w'], 'L0_ffn_w_gate': _L0_ffn_in['w_gate'], 'L0_ffn_w_up': _L0_ffn_in['w_up'], 'L0_ffn_w_down': _L0_ffn_in['w_down']}

def reference(x, ctx_2048, g_xattn, g_ffn, L0_xattn_time_decay, L0_xattn_time_first, L0_ffn_gate_w, L0_ffn_w_gate, L0_ffn_w_up, L0_ffn_w_down):
    import jax
    import jax.numpy as jnp

    def _L0_xattn_ref(batch_size, seq_len, embedding_dim, time_decay, time_first, k, v):
        import jax, jax.numpy as jnp
        import numpy as np

        def _wkv(time_decay, time_first, k, v):
            w = -jnp.exp(time_decay)
            u = time_first
            B, T, C = k.shape
            aa = jnp.zeros((B, C), dtype=k.dtype)
            bb = jnp.zeros((B, C), dtype=k.dtype)
            pp = jnp.full((B, C), -1e+38, dtype=k.dtype)

            def step(carry, kv_t):
                aa, bb, pp = carry
                kt, vt = kv_t
                ww = u + kt
                q = jnp.maximum(pp, ww)
                e1 = jnp.exp(pp - q)
                e2 = jnp.exp(ww - q)
                y_t = (e1 * aa + e2 * vt) / (e1 * bb + e2)
                ww2 = pp + w
                q2 = jnp.maximum(ww2, kt)
                e1b = jnp.exp(ww2 - q2)
                e2b = jnp.exp(kt - q2)
                new_carry = (e1b * aa + e2b * vt, e1b * bb + e2b, q2)
                return (new_carry, y_t)
            ks = jnp.transpose(k, (1, 0, 2))
            vs = jnp.transpose(v, (1, 0, 2))
            _, ys = jax.lax.scan(step, (aa, bb, pp), (ks, vs))
            return jnp.transpose(ys, (1, 0, 2))
        assert seq_len <= 128
        return _wkv(time_decay, time_first, k, v)

    def _L0_ffn_ref(x, gate_w, w_gate, w_up, w_down):
        import jax, jax.numpy as jnp
        import numpy as np
        B, S, D = (2, 256, 256)
        MOE_D = 176
        E = 16
        K = 6
        ALPHA = 0.001

        def _moe_forward(x, gate_w, w_gate, w_up, w_down):
            b, s, d = x.shape
            T = b * s
            h = x.reshape(T, d)
            logits = h @ gate_w.T
            scores = jax.nn.softmax(logits.astype(jnp.float32), axis=-1)
            topk_w, topk_idx = jax.lax.top_k(scores, K)
            cw = jnp.zeros((T, E), jnp.float32)
            cw = cw.at[jnp.arange(T)[:, None], topk_idx].add(topk_w)
            y = jnp.zeros((T, d), x.dtype)
            for e in range(E):
                g = h @ w_gate[e].T
                u = h @ w_up[e].T
                out = jax.nn.silu(g) * u @ w_down[e].T
                y = y + cw[:, e:e + 1].astype(x.dtype) * out
            counts = jnp.sum(jax.nn.one_hot(topk_idx.reshape(b, s * K), E, dtype=jnp.float32), axis=1)
            ce = counts * (E / (s * K))
            scores_bse = scores.reshape(b, s, E)
            aux = jnp.mean(jnp.sum(ce * scores_bse.mean(axis=1), axis=1)) * ALPHA
            return (y.reshape(b, s, d), aux)
        y, _aux = _moe_forward(x, gate_w, w_gate, w_up, w_down)
        return y
    x = x + jnp.tanh(g_xattn[0]) * _L0_xattn_ref(16, 128, 256, L0_xattn_time_decay, L0_xattn_time_first, _layernorm(x, axis=-1), ctx_2048)
    x = x + jnp.tanh(g_ffn[0]) * _L0_ffn_ref(_layernorm(x, axis=-1), L0_ffn_gate_w, L0_ffn_w_gate, L0_ffn_w_up, L0_ffn_w_down)
    return x

_drawn_inputs = setup_inputs


def setup_inputs(seed=0):
    import zlib

    import numpy as np

    out = dict(_drawn_inputs(seed))
    spreads = {}
    factors = {}
    for name, (base, spread) in spreads.items():
        noise = np.random.default_rng([zlib.crc32(name.encode()), seed]).standard_normal(out[name].shape)
        drawn = base * np.exp(spread * noise) if base else spread * noise
        out[name] = jnp.asarray(drawn.astype(out[name].dtype))
    for name, factor in factors.items():
        out[name] = (out[name] * factor).astype(out[name].dtype)
    return out
```

```python
from contextlib import ExitStack

import concourse.bass as bass
from concourse import mybir

F32 = mybir.dt.float32
F32R = mybir.dt.float32r
ALU = mybir.AluOpType
ACT = mybir.ActivationFunctionType
AX = mybir.AxisListType

P = 128
SEQS, STEPS, CH = 16, 128, 256
EXPERTS, FEAT, TOPK = 16, 176, 6
CC = CH // P
TT = 4
TOK = TT * STEPS
BLOCKS = SEQS * STEPS // TOK
TILES = EXPERTS * FEAT // P
WCOLS = 3 * CH
STAGE = 2
PAD = EXPERTS + 2
EPS = 1e-5
EARLY = 8
LO = 32


class Signal:

    def __init__(self, sem, per):
        self.sem, self.per = sem, per

    def at(self, b, k):
        return b * self.per + k


def first(b):
    return isinstance(b, int) and b == 0


def program(nc, x_tok, x_chan, v_chan, w_all, gate_w, decay_u, gates, out):
    with ExitStack() as ctx:
        def sb(name, shape, dt=F32):
            return ctx.enter_context(nc.sbuf_tensor(name, shape, dt))

        def signal(name, per=1):
            return Signal(ctx.enter_context(nc.semaphore(name)), per)

        w_hi = sb("w_hi", [P, TILES, WCOLS], F32R)
        w_lo = sb("w_lo", [P, TILES, WCOLS], F32R)
        w_raw = sb("w_raw", [P, STAGE, WCOLS])
        owner = sb("owner", [LO + EXPERTS, TILES * P], F32R)
        xk = sb("xk", [P, TT, CH])
        v_ev2 = sb("v_ev2", [P, CC, TOK])
        x_x1 = sb("x_x1", [P, CC, TOK])
        e1_b = sb("e1_b", [P, TOK * CC])
        e2_den = sb("e2_den", [P, CC, TOK])
        ev_a = sb("ev_a", [P, TOK * CC])
        decay = sb("decay", [P, CC, TT, STEPS])
        x1 = sb("x1", [P, CC, TOK])
        h_hi = sb("h_hi", [P, CC, TOK], F32R)
        h_lo = sb("h_lo", [P, CC, TOK], F32R)
        a32 = sb("a32", [P, 2, TOK])
        a_hi = sb("a_hi", [P, 2, TOK], F32R)
        a_lo = sb("a_lo", [P, 2, TOK], F32R)
        cw_split = sb("cw_split", [LO + EXPERTS, TOK], F32R)
        ident = sb("ident", [P, P])
        gw = sb("gw", [P, CC, EXPERTS])
        params = sb("params", [P, 2, CC])
        g_raw = sb("g_raw", [P, 2])
        g_tanh = sb("g_tanh", [P, 2])
        decay_col = sb("decay_col", [P, 2, CC])
        u_min = sb("u_min", [P, CC])
        u_max = sb("u_max", [P, CC])
        c1 = sb("c1", [P, CC])
        eps_col = sb("eps_col", [P, 1])
        carrier = sb("carrier", [P, 1])
        v0 = sb("v0", [P, CC * TT])
        bn = sb("bn", [P, TT, 6])
        mv = sb("mv", [P, TT, 2])
        sd = sb("sd", [P, TT])
        rs = sb("rs", [P, TT])
        bn2 = sb("bn2", [P, TT, 6])
        mv2 = sb("mv2", [P, TT, 2])
        sd2 = sb("sd2", [P, TT])
        rs2 = sb("rs2", [P, TT])
        lmax = sb("lmax", [P, TT])
        lsub = sb("lsub", [P, TT, EXPERTS])
        ex = sb("ex", [P, TT, PAD])
        esum = sb("esum", [P, TT])
        rsum = sb("rsum", [P, TT])
        top = sb("top", [P, TT, 8])
        rest = sb("rest", [P, TT, PAD])
        cw = sb("cw", [P, TT, EXPERTS])

        h32 = ev_a[:, :].rearrange("p (c t) -> p c t", c=CC)
        tokm = e1_b[:, :].rearrange("p (n c) -> p n c", n=TT)
        cw32 = e2_den[0:EXPERTS, 0, :]
        a_seq = ev_a[:, :].rearrange("p (s t) -> p s t", t=STEPS)
        b_seq = e1_b[:, :].rearrange("p (s t) -> p s t", t=STEPS)
        num_seq = v_ev2[:, :, :].rearrange("p c (s t) -> p (c s) t", t=STEPS)
        den_seq = e2_den[:, :, :].rearrange("p c (s t) -> p (c s) t", t=STEPS)

        ps_gate = ctx.enter_context(nc.psum_tensor("ps_gate", [P, 2, TOK], F32))
        ps_up = ctx.enter_context(nc.psum_tensor("ps_up", [P, 2, TOK], F32))
        ps_cw = ctx.enter_context(nc.psum_tensor("ps_cw", [P, TOK], F32))
        ps_y = ctx.enter_context(nc.psum_tensor("ps_y", [P, CC, TOK], F32))
        ps_mix = ctx.enter_context(nc.psum_tensor("ps_mix", [P, TOK], F32))

        params_in = signal("params_in")
        w_in = [signal(f"w_in{i}") for i in range(STAGE)]
        w_hi_ready, w_lo_ready = signal("w_hi_ready"), signal("w_lo_ready")
        ident_zero, ident_ready, owner_ready = signal("ident_zero"), signal("ident_ready"), signal("owner_ready")
        owner_draft = signal("owner_draft")
        dve_const, decay_exp, u_ready = signal("dve_const"), signal("decay_exp"), signal("u_ready")
        act_const = signal("act_const")
        xk_in, v_in, x_in = signal("xk_in", 16), signal("v_in", 16), signal("x_in", 16)
        k_bn, k_mv, k_sd, k_rs, k_norm = (signal("k_bn", TT), signal("k_mv", TT), signal("k_sd"),
                                          signal("k_rs"), signal("k_norm", TT))
        k_turned, k_copied = signal("k_turned", CC), signal("k_copied", CC)
        e1_ready, e2_ready, ev_ready, ev2_ready = (signal("e1_ready"), signal("e2_ready", CC),
                                                   signal("ev_ready"), signal("ev2_ready"))
        v0_kept, sum_a, sum_b = signal("v0_kept"), signal("sum_a"), signal("sum_b")
        num_ready, den_ready, rden_ready = signal("num_ready", CC), signal("den_ready", CC), signal("rden_ready", 4)
        y_ready, y0_ready, x1_new = signal("y_ready"), signal("y0_ready"), signal("x1_new")
        x1_turned, x1_copied = signal("x1_turned", 2), signal("x1_copied", 2)
        h_bn, h_mv, h_sd, h_rs, h_norm = (signal("h_bn", TT), signal("h_mv", TT), signal("h_sd"),
                                          signal("h_rs"), signal("h_norm", TT))
        h_turned, h_ready, logits_ready = signal("h_turned", CC), signal("h_ready", CC), signal("logits_ready")
        lmax_ready, lsub_ready, ex_ready = signal("lmax_ready"), signal("lsub_ready"), signal("ex_ready")
        esum_ready, rsum_ready, top_ready, top_cut = (signal("esum_ready"), signal("rsum_ready"),
                                                      signal("top_ready", TT), signal("top_cut"))
        rest_ready, cw_raw, cw_ready = signal("rest_ready", TT), signal("cw_raw"), signal("cw_ready")
        cw_turned, cw_copied = signal("cw_turned"), signal("cw_copied")
        h_hi_ready, h_lo_ready = signal("h_hi_ready", CC), signal("h_lo_ready", CC)
        cw_hi_ready, cw_lo_ready, x1_kept = signal("cw_hi_ready"), signal("cw_lo_ready"), signal("x1_kept")
        gate_done, up_done, cw_spread = signal("gate_done", TILES), signal("up_done", TILES), signal("cw_spread", TILES)
        silu_ready, gu_ready, act_ready = signal("silu_ready", TILES), signal("gu_ready", TILES), signal("act_ready", TILES)
        a_hi_ready, a_lo_ready, down_done = signal("a_hi_ready", TILES), signal("a_lo_ready", TILES), signal("down_done", TILES)
        out_ready, stored = signal("out_ready"), signal("stored", 16)

        block = ctx.enter_context(nc.Block())

        @block.sync
        def _(sp):
            sp.dma_start(params[:, :, :], decay_u).then_inc(params_in.sem, 16)
            sp.dma_start(gw[:, :, :], gate_w).then_inc(params_in.sem, 16)
            sp.dma_start(g_raw[:, 0:1], gates[0:1].partition_broadcast(P)).then_inc(params_in.sem, 16)
            sp.dma_start(g_raw[:, 1:2], gates[1:2].partition_broadcast(P)).then_inc(params_in.sem, 16)
            for j in range(TILES):
                if j >= STAGE:
                    sp.wait_ge(w_hi_ready.sem, j - STAGE + 1)
                    sp.wait_ge(w_lo_ready.sem, j - STAGE + 1)
                sp.dma_start(w_raw[:, j % STAGE, :], w_all[j]).then_inc(w_in[j % STAGE].sem, 16)
            with sp.Fori(0, BLOCKS) as b:
                sp.wait_ge(out_ready.sem, out_ready.at(b, 1))
                sp.dma_start(out[bass.ds(b, 1)].rearrange("a p n -> (a p) n"),
                             x1[:, :, :].rearrange("p c t -> p (c t)")).then_inc(stored.sem, 16)
            sp.wait_ge(stored.sem, stored.at(BLOCKS, 0))

        @block.tensor
        def _(pe):
            def product(dst, lhs, rhs, start, stop):
                n = len(lhs)
                for i in range(n):
                    (l_hi, l_lo), (r_hi, r_lo) = lhs[i], rhs[i]
                    nc.tensor.matmul(dst, l_hi, r_hi, start=start and i == 0, stop=False)
                    nc.tensor.matmul(dst, l_hi, r_lo, start=False, stop=False)
                    last = nc.tensor.matmul(dst, l_lo, r_hi, start=False, stop=stop and i == n - 1)
                return last

            def weights(j, part, n=CC):
                cols = [slice(part * CH + c * P, part * CH + (c + 1) * P) for c in range(n)]
                return [(w_hi[:, j, s], w_lo[:, j, s]) for s in cols]

            h_pairs = [(h_hi[:, c, :], h_lo[:, c, :]) for c in range(CC)]

            def turn_k(b, c):
                if c == 0:
                    pe.wait_ge(k_norm.sem, k_norm.at(b, TT))
                    if not first(b):
                        pe.wait_ge(cw_copied.sem, cw_copied.at(b, 0))
                else:
                    pe.wait_ge(k_copied.sem, k_copied.at(b, c))
                for n in range(TT):
                    mm = nc.tensor.transpose(ps_mix[:, n * P:(n + 1) * P], xk[:, n, c * P:(c + 1) * P], ident[:, :])
                mm.then_inc(k_turned.sem, 1)

            def turn_x1(b, half):
                if half == 0:
                    pe.wait_ge(x1_new.sem, x1_new.at(b, 1))
                else:
                    pe.wait_ge(x1_copied.sem, x1_copied.at(b, 1))
                for i in range(2):
                    n = 2 * half + i
                    for c in range(CC):
                        mm = nc.tensor.transpose(ps_mix[:, i * CH + c * P:i * CH + (c + 1) * P],
                                                 x_x1[:, c, n * P:(n + 1) * P], ident[:, :])
                mm.then_inc(x1_turned.sem, 1)

            def turn_h(b, c):
                if c == 0:
                    pe.wait_ge(h_norm.sem, h_norm.at(b, TT))
                    pe.wait_ge(x1_copied.sem, x1_copied.at(b, 2))
                else:
                    pe.wait_ge(h_ready.sem, h_ready.at(b, c))
                for n in range(TT):
                    mm = nc.tensor.transpose(ps_mix[:, n * P:(n + 1) * P], tokm[:, n, c * P:(c + 1) * P], ident[:, :])
                mm.then_inc(h_turned.sem, 1)

            def logits(b):
                pe.wait_ge(h_ready.sem, h_ready.at(b, CC))
                for n in range(TT):
                    for c in range(CC):
                        mm = nc.tensor.matmul(ps_mix[:, n * EXPERTS:(n + 1) * EXPERTS],
                                              h32[:, c, n * P:(n + 1) * P], gw[:, c, :],
                                              start=(c == 0), stop=(c == CC - 1))
                mm.then_inc(logits_ready.sem, 1)

            def turn_cw(b):
                pe.wait_ge(cw_ready.sem, cw_ready.at(b, 1))
                for n in range(TT):
                    mm = nc.tensor.transpose(ps_mix[0:EXPERTS, n * P:(n + 1) * P], cw[:, n, :], ident[:, :])
                mm.then_inc(cw_turned.sem, 1)

            def mix(b, slot, half):
                if slot == 2:
                    turn_k(b, half)
                if slot == 15:
                    turn_x1(b, half)
                if slot == 18:
                    turn_h(b, half)
                if slot == 19 and half == 0:
                    logits(b)
                if slot == 21 and half == 0:
                    turn_cw(b)

            def down(b, j):
                n = b * TILES + j
                pe.wait_ge(a_hi_ready.sem, n + 1)
                pe.wait_ge(a_lo_ready.sem, n + 1)
                if j == 0 and not first(b):
                    pe.wait_ge(out_ready.sem, out_ready.at(b, 0))
                for c in range(CC):
                    mm = product(ps_y[:, c, :], [weights(j, 2)[c]],
                                 [(a_hi[:, j % 2, :], a_lo[:, j % 2, :])], start=(j == 0), stop=(j == TILES - 1))
                mm.then_inc(down_done.sem, 1)

            def experts(b, ahead):
                for j in range(TILES):
                    n = b * TILES + j
                    if first(b):
                        pe.wait_ge(w_hi_ready.sem, j + 1)
                        pe.wait_ge(w_lo_ready.sem, j + 1)
                    if j == 0:
                        pe.wait_ge(h_hi_ready.sem, h_hi_ready.at(b, CC))
                        pe.wait_ge(h_lo_ready.sem, h_lo_ready.at(b, CC))
                    if not (first(b) and j < 2):
                        pe.wait_ge(silu_ready.sem, n - 1)
                    product(ps_gate[:, j % 2, :], weights(j, 0), h_pairs, True, True).then_inc(gate_done.sem, 1)
                    if not (first(b) and j < 2):
                        pe.wait_ge(gu_ready.sem, n - 1)
                    product(ps_up[:, j % 2, :], weights(j, 1), h_pairs, True, True).then_inc(up_done.sem, 1)
                    if j == 0:
                        pe.wait_ge(cw_hi_ready.sem, cw_hi_ready.at(b, 1))
                        pe.wait_ge(cw_lo_ready.sem, cw_lo_ready.at(b, 1))
                    if first(b) and j == 0:
                        pe.wait_ge(owner_ready.sem, 3)
                    if not (first(b) and j == 0):
                        pe.wait_ge(act_ready.sem, n)
                    nc.tensor.matmul(ps_cw[:, :], owner[:, j * P:(j + 1) * P], cw_split[:, :],
                                     start=True, stop=True).then_inc(cw_spread.sem, 1)
                    if ahead:
                        mix(b + 1, j, 0)
                    if j >= 2:
                        down(b, j - 2)
                    if ahead:
                        mix(b + 1, j, 1)
                down(b, TILES - 2)
                down(b, TILES - 1)

            pe.wait_ge(ident_ready.sem, 1)
            for slot in range(TILES):
                if slot == 19:
                    pe.wait_ge(params_in.sem, 64)
                mix(0, slot, 0)
                mix(0, slot, 1)
            experts(0, True)
            with pe.Fori(1, BLOCKS - 1) as b:
                experts(b, True)
            experts(BLOCKS - 1, False)

        @block.scalar
        def _(act):
            def load(b, dst, src, sem):
                act.dma_start(dst, src[bass.ds(b, 1)].rearrange("a p n -> (a p) n")).then_inc(sem, 16)

            def load_xk(b):
                load(b, xk[:, :, :].rearrange("p n c -> p (n c)"), x_tok, xk_in.sem)

            def load_v(b):
                load(b, v_ev2[:, :, :].rearrange("p c t -> p (c t)"), v_chan, v_in.sem)

            def load_x(b):
                load(b, x_x1[:, :, :].rearrange("p c t -> p (c t)"), x_chan, x_in.sem)

            def split_w(j):
                act.wait_ge(w_in[j % STAGE].sem, 16 * (j // STAGE + 1))
                nc.scalar.copy(w_hi[:, j, :], w_raw[:, j % STAGE, :]).then_inc(w_hi_ready.sem, 1)

            def copy_k(b, c):
                act.wait_ge(k_turned.sem, k_turned.at(b, c + 1))
                if c == 0 and not first(b):
                    act.wait_ge(cw_lo_ready.sem, cw_lo_ready.at(b, 0))
                nc.scalar.copy(e2_den[:, c, :], ps_mix[:, :]).then_inc(k_copied.sem, 1)

            def exps(b):
                act.wait_ge(k_copied.sem, k_copied.at(b, CC))
                nc.scalar.activation(e1_b[:, :], e2_den[:, :, :].rearrange("p c t -> p (c t)"),
                                     ACT.Exp).then_inc(e1_ready.sem, 1)
                act.wait_ge(e1_ready.sem, e1_ready.at(b, 1))
                for c in range(CC):
                    nc.scalar.activation(e2_den[:, c, :], e2_den[:, c, :], ACT.Exp,
                                         bias=u_min[:, c:c + 1]).then_inc(e2_ready.sem, 1)

            def deviation(b, var, dst, ready, done):
                act.wait_ge(ready.sem, ready.at(b, TT))
                nc.scalar.activation(dst, var, ACT.Sqrt, bias=eps_col[:, 0:1]).then_inc(done.sem, 1)

            def mix(b, slot, half, more):
                if slot == 0 and half == 1:
                    deviation(b, mv[:, :, 1], sd[:, :], k_mv, k_sd)
                if slot == 2:
                    copy_k(b, half)
                    if half == 1 and more:
                        load_xk(b + 1)
                if slot == 3 and half == 1:
                    exps(b)
                if slot == 15:
                    act.wait_ge(x1_turned.sem, x1_turned.at(b, half + 1))
                    if half == 0 and more:
                        load_v(b + 1)
                    nc.scalar.copy(e1_b[:, half * TOK:(half + 1) * TOK], ps_mix[:, :]).then_inc(x1_copied.sem, 1)
                if slot == 16 and half == 1:
                    deviation(b, mv2[:, :, 1], sd2[:, :], h_mv, h_sd)
                if slot == 18:
                    act.wait_ge(h_turned.sem, h_turned.at(b, half + 1))
                    nc.scalar.copy(h32[:, half, :], ps_mix[:, :]).then_inc(h_ready.sem, 1)
                if slot == 19 and half == 1:
                    act.wait_ge(lsub_ready.sem, lsub_ready.at(b, 1))
                    nc.scalar.activation(ex[:, :, 0:EXPERTS], lsub[:, :, :], ACT.Exp).then_inc(ex_ready.sem, 1)
                if slot == 21 and half == 1:
                    act.wait_ge(cw_turned.sem, cw_turned.at(b, 1))
                    nc.scalar.copy(cw32, ps_mix[0:EXPERTS, :]).then_inc(cw_copied.sem, 1)

            def hand_over(b):
                if not first(b):
                    act.wait_ge(up_done.sem, up_done.at(b, 0))
                act.wait_ge(h_ready.sem, h_ready.at(b, CC))
                for c in range(CC):
                    nc.scalar.copy(h_hi[:, c, :], h32[:, c, :]).then_inc(h_hi_ready.sem, 1)
                if not first(b):
                    act.wait_ge(cw_spread.sem, cw_spread.at(b, 0))
                act.wait_ge(cw_copied.sem, cw_copied.at(b, 1))
                nc.scalar.copy(cw_split[0:EXPERTS, :], cw32).then_inc(cw_hi_ready.sem, 1)

            def keep_x1(b):
                if first(b):
                    act.wait_ge(owner_ready.sem, 3)
                else:
                    act.wait_ge(stored.sem, stored.at(b, 0))
                act.wait_ge(x1_copied.sem, x1_copied.at(b, 2))
                nc.scalar.copy(x1[:, :, :].rearrange("p c t -> p (c t)"),
                               x_x1[:, :, :].rearrange("p c t -> p (c t)")).then_inc(x1_kept.sem, 1)

            def experts(b, ahead, more):
                for j in range(TILES):
                    n = b * TILES + j
                    act.wait_ge(gate_done.sem, n + 1)
                    if not (first(b) and j < 2):
                        act.wait_ge(a_lo_ready.sem, n - 1)
                    nc.scalar.activation(a32[:, j % 2, :], ps_gate[:, j % 2, :], ACT.Silu).then_inc(silu_ready.sem, 1)
                    if first(b) and j + EARLY < TILES:
                        split_w(j + EARLY)
                    if ahead:
                        mix(b + 1, j, 0, more)
                    act.wait_ge(act_ready.sem, n + 1)
                    if not (first(b) and j < 2):
                        act.wait_ge(down_done.sem, n - 1)
                    nc.scalar.copy(a_hi[:, j % 2, :], a32[:, j % 2, :]).then_inc(a_hi_ready.sem, 1)
                    if ahead:
                        mix(b + 1, j, 1, more)
                    if j == 2:
                        keep_x1(b)
                        if ahead:
                            act.wait_ge(x1_kept.sem, x1_kept.at(b, 1))
                            load_x(b + 1)

            load_xk(0)
            load_v(0)
            load_x(0)
            act.wait_ge(params_in.sem, 64)
            nc.scalar.activation(g_tanh[:, :], g_raw[:, :], ACT.Tanh).then_inc(act_const.sem, 1)
            nc.scalar.activation(decay_col[:, 0, :], params[:, 0, :], ACT.Exp).then_inc(decay_exp.sem, 1)
            act.wait_ge(decay_exp.sem, 1)
            nc.scalar.activation(decay_col[:, 1, :], decay_col[:, 0, :], ACT.Exp, scale=-1.0).then_inc(act_const.sem, 1)
            act.wait_ge(u_ready.sem, 2)
            nc.scalar.activation(c1[:, :], u_max[:, :], ACT.Exp, scale=-1.0).then_inc(act_const.sem, 1)
            act.wait_ge(dve_const.sem, 1)
            for slot in range(TILES):
                mix(0, slot, 0, True)
                mix(0, slot, 1, True)
                if 5 <= slot < 5 + EARLY:
                    split_w(slot - 5)
            hand_over(0)
            experts(0, True, True)
            hand_over(1)
            with act.Fori(1, BLOCKS - 2) as b:
                experts(b, True, True)
                hand_over(b + 1)
            experts(BLOCKS - 2, True, False)
            hand_over(BLOCKS - 1)
            experts(BLOCKS - 1, False, False)

        @block.gpsimd
        def _(pool):
            nc.gpsimd.memset(ident[:, :], 0.0).then_inc(ident_zero.sem, 1)
            pool.wait_ge(ident_zero.sem, 1)
            nc.gpsimd.affine_select(out=ident[:, :], in_=ident[:, :], compare_op=ALU.not_equal, fill=1.0, base=0,
                                    pattern=[[-1, P]], channel_multiplier=1).then_inc(ident_ready.sem, 1)
            step = 0
            for f0 in range(0, TILES * P, CC * TOK):
                width = min(CC * TOK, TILES * P - f0)
                draft = x1[:, :, :].rearrange("p c t -> p (c t)")[0:LO + EXPERTS, 0:width]
                if step:
                    pool.wait_ge(owner_ready.sem, f0 // (CC * TOK))
                nc.gpsimd.memset(draft, 1.0).then_inc(owner_draft.sem, 1)
                step += 1
                for start in (0, LO):
                    rows = draft[start:start + EXPERTS, :]
                    for base, sign in ((f0, 1), (FEAT - 1 - f0, -1)):
                        pool.wait_ge(owner_draft.sem, step)
                        nc.gpsimd.affine_select(out=rows, in_=rows, compare_op=ALU.is_ge, fill=0.0, base=base,
                                                pattern=[[sign, width]],
                                                channel_multiplier=-sign * FEAT).then_inc(owner_draft.sem, 1)
                        step += 1
                pool.wait_ge(owner_draft.sem, step)
                nc.gpsimd.tensor_copy(owner[:, f0:f0 + width], draft).then_inc(owner_ready.sem, 1)

            def split_w(j):
                pool.wait_ge(w_hi_ready.sem, j + 1)
                nc.gpsimd.tensor_tensor(w_lo[:, j, :], w_raw[:, j % STAGE, :], w_hi[:, j, :].bitcast(F32),
                                        ALU.subtract).then_inc(w_lo_ready.sem, 1)

            def mix(b):
                pool.wait_ge(v_in.sem, v_in.at(b, 16))
                pool.wait_ge(e2_ready.sem, e2_ready.at(b, CC))
                pool.wait_ge(ev_ready.sem, ev_ready.at(b, 1))
                pool.wait_ge(v0_kept.sem, v0_kept.at(b, 1))
                nc.gpsimd.tensor_tensor(v_ev2[:, :, :], e2_den[:, :, :], v_ev2[:, :, :],
                                        ALU.mult).then_inc(ev2_ready.sem, 1)

            def experts(b, ahead):
                for j in range(TILES):
                    n = b * TILES + j
                    if ahead and j == 5:
                        mix(b + 1)
                    pool.wait_ge(a_hi_ready.sem, n + 1)
                    if not (first(b) and j < 2):
                        pool.wait_ge(down_done.sem, n - 1)
                    nc.gpsimd.tensor_tensor(a_lo[:, j % 2, :], a32[:, j % 2, :], a_hi[:, j % 2, :].bitcast(F32),
                                            ALU.subtract).then_inc(a_lo_ready.sem, 1)
                    if first(b) and j + EARLY < TILES:
                        split_w(j + EARLY)

            mix(0)
            for j in range(EARLY):
                split_w(j)
            experts(0, True)
            with pool.Fori(1, BLOCKS - 1) as b:
                experts(b, True)
            experts(BLOCKS - 1, False)

        @block.vector
        def _(dve):
            def statistics(b, src, bn_, mv_, bn_sem, mv_sem):
                for n in range(TT):
                    nc.vector.bn_stats(bn_[:, n, :], src[:, n, :]).then_inc(bn_sem.sem, 1)
                dve.wait_ge(bn_sem.sem, bn_sem.at(b, TT))
                nc.vector.memset(carrier[:, :], 0.0)
                for n in range(TT):
                    nc.vector.bn_aggr(mv_[:, n, :], bn_[:, n, :]).then_inc(mv_sem.sem, 1)

            def normalise(b, data, mv_, sd_, rs_, sd_sem, rs_sem, mv_sem, norm_sem):
                dve.wait_ge(sd_sem.sem, sd_sem.at(b, 1))
                nc.vector.reciprocal(rs_[:, :], sd_[:, :]).then_inc(rs_sem.sem, 1)
                dve.wait_ge(rs_sem.sem, rs_sem.at(b, 1))
                dve.wait_ge(mv_sem.sem, mv_sem.at(b, TT))
                for n in range(TT):
                    nc.vector.tensor_scalar(data[:, n, :], data[:, n, :], mv_[:, n, 0:1], rs_[:, n:n + 1],
                                            ALU.subtract, ALU.mult).then_inc(norm_sem.sem, 1)

            def mix(b, slot):
                if slot == 0:
                    dve.wait_ge(xk_in.sem, xk_in.at(b, 16))
                    statistics(b, xk, bn, mv, k_bn, k_mv)
                if slot == 1:
                    normalise(b, xk, mv, sd, rs, k_sd, k_rs, k_mv, k_norm)
                if slot == 4:
                    dve.wait_ge(v_in.sem, v_in.at(b, 16))
                    nc.vector.tensor_copy(v0[:, :], num_seq[:, :, 0]).then_inc(v0_kept.sem, 1)
                    dve.wait_ge(e1_ready.sem, e1_ready.at(b, 1))
                    nc.vector.tensor_tensor(ev_a[:, :], e1_b[:, :], v_ev2[:, :, :].rearrange("p c t -> p (c t)"),
                                            ALU.mult).then_inc(ev_ready.sem, 1)
                if slot == 5:
                    dve.wait_ge(ev_ready.sem, ev_ready.at(b, 1))
                    nc.vector.tensor_tensor_scan(ev_a[:, :], decay[:, :, :, :].rearrange("p c s t -> p (c s t)"),
                                                 ev_a[:, :], 0.0, ALU.mult, ALU.add).then_inc(sum_a.sem, 1)
                if slot == 6:
                    nc.vector.tensor_tensor_scan(e1_b[:, :], decay[:, :, :, :].rearrange("p c s t -> p (c s t)"),
                                                 e1_b[:, :], 0.0, ALU.mult, ALU.add).then_inc(sum_b.sem, 1)
                if slot in (7, 8):
                    if slot == 7:
                        dve.wait_ge(ev2_ready.sem, ev2_ready.at(b, 1))
                        dve.wait_ge(sum_a.sem, sum_a.at(b, 1))
                        sums, dst, done = a_seq, num_seq, num_ready
                    else:
                        dve.wait_ge(sum_b.sem, sum_b.at(b, 1))
                        sums, dst, done = b_seq, den_seq, den_ready
                    for c in range(CC):
                        s = slice(c * TT, (c + 1) * TT)
                        nc.vector.scalar_tensor_tensor(dst[:, s, 1:STEPS], sums[:, s, 0:STEPS - 1], c1[:, c:c + 1],
                                                       dst[:, s, 1:STEPS], ALU.mult, ALU.add).then_inc(done.sem, 1)
                if 9 <= slot < 13:
                    if slot == 9:
                        dve.wait_ge(den_ready.sem, den_ready.at(b, CC))
                    s = slice(2 * (slot - 9), 2 * (slot - 8))
                    nc.vector.reciprocal(den_seq[:, s, 1:STEPS], den_seq[:, s, 1:STEPS]).then_inc(rden_ready.sem, 1)
                if slot == 13:
                    dve.wait_ge(rden_ready.sem, rden_ready.at(b, 4))
                    dve.wait_ge(num_ready.sem, num_ready.at(b, CC))
                    nc.vector.tensor_tensor(num_seq[:, :, 1:STEPS], num_seq[:, :, 1:STEPS], den_seq[:, :, 1:STEPS],
                                            ALU.mult).then_inc(y_ready.sem, 1)
                    dve.wait_ge(v0_kept.sem, v0_kept.at(b, 1))
                    nc.vector.tensor_copy(num_seq[:, :, 0], v0[:, :]).then_inc(y0_ready.sem, 1)
                if slot == 14:
                    dve.wait_ge(y_ready.sem, y_ready.at(b, 1))
                    dve.wait_ge(y0_ready.sem, y0_ready.at(b, 1))
                    dve.wait_ge(x_in.sem, x_in.at(b, 16))
                    nc.vector.scalar_tensor_tensor(x_x1[:, :, :], v_ev2[:, :, :], g_tanh[:, 0:1], x_x1[:, :, :],
                                                   ALU.mult, ALU.add).then_inc(x1_new.sem, 1)
                if slot == 16:
                    dve.wait_ge(x1_copied.sem, x1_copied.at(b, 2))
                    statistics(b, tokm, bn2, mv2, h_bn, h_mv)
                if slot == 17:
                    normalise(b, tokm, mv2, sd2, rs2, h_sd, h_rs, h_mv, h_norm)
                if slot == 19:
                    dve.wait_ge(logits_ready.sem, logits_ready.at(b, 1))
                    rows = ps_mix[:, 0:TT * EXPERTS].rearrange("p (n e) -> p n e", n=TT)
                    nc.vector.tensor_reduce(lmax[:, :], rows, AX.X, ALU.max).then_inc(lmax_ready.sem, 1)
                    dve.wait_ge(lmax_ready.sem, lmax_ready.at(b, 1))
                    nc.vector.tensor_tensor(lsub[:, :, :], rows, lmax[:, :].unsqueeze(2).to_broadcast([P, TT, EXPERTS]),
                                            ALU.subtract).then_inc(lsub_ready.sem, 1)
                if slot == 20:
                    dve.wait_ge(ex_ready.sem, ex_ready.at(b, 1))
                    nc.vector.tensor_reduce(esum[:, :], ex[:, :, 0:EXPERTS], AX.X, ALU.add).then_inc(esum_ready.sem, 1)
                    for n in range(TT):
                        nc.vector.max(top[:, n, :], ex[:, n, :]).then_inc(top_ready.sem, 1)
                    dve.wait_ge(top_ready.sem, top_ready.at(b, TT))
                    nc.vector.memset(top[:, :, TOPK:8], -1.0).then_inc(top_cut.sem, 1)
                    dve.wait_ge(top_cut.sem, top_cut.at(b, 1))
                    dve.wait_ge(esum_ready.sem, esum_ready.at(b, 1))
                    nc.vector.reciprocal(rsum[:, :], esum[:, :]).then_inc(rsum_ready.sem, 1)
                    for n in range(TT):
                        nc.vector.match_replace(rest[:, n, :], top[:, n, :], ex[:, n, :], 0.0).then_inc(rest_ready.sem, 1)
                    dve.wait_ge(rest_ready.sem, rest_ready.at(b, TT))
                    nc.vector.tensor_tensor(cw[:, :, :], ex[:, :, 0:EXPERTS], rest[:, :, 0:EXPERTS],
                                            ALU.subtract).then_inc(cw_raw.sem, 1)
                    dve.wait_ge(cw_raw.sem, cw_raw.at(b, 1))
                    dve.wait_ge(rsum_ready.sem, rsum_ready.at(b, 1))
                    nc.vector.tensor_tensor(cw[:, :, :], cw[:, :, :], rsum[:, :].unsqueeze(2).to_broadcast([P, TT, EXPERTS]),
                                            ALU.mult).then_inc(cw_ready.sem, 1)

            def hand_over(b):
                for c in range(CC):
                    dve.wait_ge(h_hi_ready.sem, h_hi_ready.at(b, c + 1))
                    nc.vector.tensor_tensor(h_lo[:, c, :], h32[:, c, :], h_hi[:, c, :].bitcast(F32),
                                            ALU.subtract).then_inc(h_lo_ready.sem, 1)
                dve.wait_ge(cw_hi_ready.sem, cw_hi_ready.at(b, 1))
                nc.vector.tensor_tensor(cw_split[LO:LO + EXPERTS, :], cw32, cw_split[0:EXPERTS, :].bitcast(F32),
                                        ALU.subtract).then_inc(cw_lo_ready.sem, 1)

            def result(b):
                dve.wait_ge(down_done.sem, down_done.at(b, TILES))
                dve.wait_ge(x1_kept.sem, x1_kept.at(b, 1))
                nc.vector.scalar_tensor_tensor(x1[:, :, :], ps_y[:, :, :], g_tanh[:, 1:2], x1[:, :, :],
                                               ALU.mult, ALU.add).then_inc(out_ready.sem, 1)

            def experts(b, ahead):
                for j in range(TILES):
                    n = b * TILES + j
                    dve.wait_ge(silu_ready.sem, n + 1)
                    dve.wait_ge(up_done.sem, n + 1)
                    nc.vector.tensor_tensor(a32[:, j % 2, :], a32[:, j % 2, :], ps_up[:, j % 2, :],
                                            ALU.mult).then_inc(gu_ready.sem, 1)
                    dve.wait_ge(gu_ready.sem, n + 1)
                    dve.wait_ge(cw_spread.sem, n + 1)
                    nc.vector.tensor_tensor(a32[:, j % 2, :], a32[:, j % 2, :], ps_cw[:, :],
                                            ALU.mult).then_inc(act_ready.sem, 1)
                    if ahead:
                        mix(b + 1, j)
                if ahead:
                    hand_over(b + 1)
                result(b)

            nc.vector.memset(eps_col[:, :], EPS).then_inc(dve_const.sem, 1)
            nc.vector.memset(decay[:, :, :, :], 0.0).then_inc(dve_const.sem, 1)
            nc.vector.memset(ex[:, :, EXPERTS:PAD], -1.0).then_inc(dve_const.sem, 1)
            nc.vector.memset(cw_split[:, :].bitcast(F32), 0.0).then_inc(dve_const.sem, 1)
            dve.wait_ge(params_in.sem, 64)
            nc.vector.tensor_scalar(u_min[:, :], params[:, 1, :], 0.0, None, ALU.min).then_inc(u_ready.sem, 1)
            nc.vector.tensor_scalar(u_max[:, :], params[:, 1, :], 0.0, None, ALU.max).then_inc(u_ready.sem, 1)
            mix(0, 0)
            dve.wait_ge(act_const.sem, 3)
            dve.wait_ge(dve_const.sem, 4)
            for c in range(CC):
                nc.vector.tensor_scalar(decay[:, c, :, 1:STEPS], decay[:, c, :, 1:STEPS], decay_col[:, 1, c:c + 1],
                                        None, ALU.add).then_inc(dve_const.sem, 1)
            mix(0, 1)
            dve.wait_ge(dve_const.sem, 4 + CC)
            for slot in range(2, TILES):
                mix(0, slot)
            hand_over(0)
            experts(0, True)
            with dve.Fori(1, BLOCKS - 1) as b:
                experts(b, True)
            experts(BLOCKS - 1, False)


def kernel(x, ctx_2048, g_xattn, g_ffn, L0_xattn_time_decay, L0_xattn_time_first,
           L0_ffn_gate_w, L0_ffn_w_gate, L0_ffn_w_up, L0_ffn_w_down):
    import numpy as np
    import concourse.bacc as bacc
    from concourse.bass_utils import run_bass_kernel_spmd

    def chan_major(a):
        a = np.asarray(a).reshape(BLOCKS, TOK, CC, P).transpose(0, 3, 2, 1)
        return np.ascontiguousarray(a).reshape(BLOCKS, P, CC * TOK)

    def row_tiles(a):
        return a.reshape(TILES, P, CC, P).transpose(0, 3, 2, 1).reshape(TILES, P, CH)

    tok = np.asarray(x).reshape(BLOCKS, TT, STEPS, CH).transpose(0, 2, 1, 3)
    w_gate, w_up, w_down = np.asarray(L0_ffn_w_gate), np.asarray(L0_ffn_w_up), np.asarray(L0_ffn_w_down)
    arrays = {
        "x_tok": np.ascontiguousarray(tok).reshape(BLOCKS, P, TT * CH),
        "x_chan": chan_major(x),
        "v_chan": chan_major(ctx_2048),
        "w_all": np.ascontiguousarray(np.concatenate(
            [row_tiles(w_gate), row_tiles(w_up), w_down.transpose(0, 2, 1).reshape(TILES, P, CH)], axis=2)),
        "gate_w": np.ascontiguousarray(np.asarray(L0_ffn_gate_w).reshape(EXPERTS, CC, P).transpose(2, 1, 0)),
        "decay_u": np.ascontiguousarray(np.stack(
            [np.asarray(L0_xattn_time_decay), np.asarray(L0_xattn_time_first)]).reshape(2, CC, P).transpose(2, 0, 1)),
        "gates": np.concatenate([np.asarray(g_xattn), np.asarray(g_ffn)]),
    }
    nc = bacc.Bacc("TRN2", target_bir_lowering=False, num_devices=1)
    args = [nc.dram_tensor(name, a.shape, mybir.dt.from_np(a.dtype), kind="ExternalInput").ap()
            for name, a in arrays.items()]
    out = nc.dram_tensor("out", (BLOCKS, P, CC * TOK), F32, kind="ExternalOutput").ap()
    program(nc, *args, out)
    r = run_bass_kernel_spmd(nc, [arrays], core_ids=[0])
    y = r.results[0]["out"].reshape(BLOCKS, P, CC, TOK).transpose(0, 3, 2, 1)
    return np.ascontiguousarray(y).reshape(SEQS, STEPS, CH)
```

```python
from contextlib import ExitStack

import concourse.bass as bass
from concourse import mybir

F32 = mybir.dt.float32
F32R = mybir.dt.float32r
ALU = mybir.AluOpType
ACT = mybir.ActivationFunctionType
AX = mybir.AxisListType

P = 128
SEQS, STEPS, CH = 16, 128, 256
EXPERTS, FEAT, TOPK = 16, 176, 6
CC = CH // P
TOKENS = SEQS * STEPS
MAIN = 384
TOK = 512
BLOCKS = (TOKENS - TOK) // MAIN + 1
TILES = EXPERTS * FEAT // P
WCOLS = 3 * CH
STAGE = 4
PAD = EXPERTS + 2
EPS = 1e-5
EARLY = 9
EARLY_LN = 5
W_FIRST = 11
RECIPS = 4


def owners(j):
    f0, f1 = j * P, (j + 1) * P
    return [(e, max(f0, e * FEAT) - f0, min(f1, (e + 1) * FEAT) - f0) for e in range(f0 // FEAT, (f1 - 1) // FEAT + 1)]


class Signal:

    def __init__(self, sem, per):
        self.sem, self.per = sem, per

    def at(self, b, k=None):
        return b * self.per + (self.per if k is None else k)


def first(b):
    return isinstance(b, int) and b == 0


def width(b):
    return TOK if isinstance(b, int) and b == BLOCKS - 1 else MAIN


def program(nc, x_tok, x_chan, v_chan, w_all, gate_w, decay_u, gates, out):
    cw_rows = nc.dram_tensor("cw_rows", (BLOCKS, EXPERTS, TOK), F32, kind="Internal").ap()

    with ExitStack() as ctx:
        def sb(name, shape, dt=F32):
            return ctx.enter_context(nc.sbuf_tensor(name, shape, dt))

        def signal(name, per=1):
            return Signal(ctx.enter_context(nc.semaphore(name)), per)

        w_hi = sb("w_hi", [P, TILES, WCOLS], F32R)
        w_lo = sb("w_lo", [P, TILES, WCOLS], F32R)
        w_raw = sb("w_raw", [P, STAGE, WCOLS])
        xk = sb("xk", [P, TOK // STEPS, CH])
        v_a = sb("v_a", [P, CC * TOK])
        x_x1 = sb("x_x1", [P, CC * TOK])
        e1_h = sb("e1_h", [P, CC * TOK])
        b_h = sb("b_h", [P, CC * TOK])
        e2_den = sb("e2_den", [P, CC * TOK])
        num_y = sb("num_y", [P, CC * TOK])
        decay = sb("decay", [P, CC * TOK])
        x1 = sb("x1", [P, CC * TOK])
        h_hi = sb("h_hi", [P, CC, TOK], F32R)
        h_lo = sb("h_lo", [P, CC, TOK], F32R)
        cw_b = sb("cw_b", [P, 2, TOK])
        a32 = sb("a32", [P, 2, TOK])
        a_hi = sb("a_hi", [P, 2, TOK], F32R)
        a_lo = sb("a_lo", [P, 2, TOK], F32R)
        ident = sb("ident", [P, P])
        gw = sb("gw", [P, CC, EXPERTS])
        params = sb("params", [P, 2, CC])
        g_raw = sb("g_raw", [P, 2])
        g_tanh = sb("g_tanh", [P, 2])
        decay_col = sb("decay_col", [P, 2, CC])
        u_min = sb("u_min", [P, CC])
        u_max = sb("u_max", [P, CC])
        c1 = sb("c1", [P, CC])
        minus_half = sb("minus_half", [P, TOK // STEPS])
        carrier = sb("carrier", [P, 1])
        v0 = sb("v0", [P, CC * TOK // STEPS])
        bn = sb("bn", [P, TOK // STEPS, 6])
        mv = sb("mv", [P, TOK // STEPS, 2])
        var_eps = sb("var_eps", [P, TOK // STEPS])
        rs = sb("rs", [P, TOK // STEPS])
        lmax = sb("lmax", [P, TOK // STEPS])
        lsub = sb("lsub", [P, TOK // STEPS, EXPERTS])
        ex = sb("ex", [P, TOK // STEPS, PAD])
        esum = sb("esum", [P, TOK // STEPS])
        rsum = sb("rsum", [P, TOK // STEPS])
        top = sb("top", [P, TOK // STEPS, 8])
        rest = sb("rest", [P, TOK // STEPS, PAD])
        cw = sb("cw", [P, TOK // STEPS, EXPERTS])

        def chan(buf, b):
            return buf[:, 0:CC * width(b)].rearrange("p (c t) -> p c t", c=CC)

        def seqs(buf, b):
            return buf[:, 0:CC * width(b)].rearrange("p (s t) -> p s t", t=STEPS)

        def flat(buf, b):
            return buf[:, 0:CC * width(b)]

        def tokm(buf, b):
            return buf[:, 0:CC * width(b)].rearrange("p (n c) -> p n c", c=CH)

        ps_gate = ctx.enter_context(nc.psum_tensor("ps_gate", [P, 2, TOK], F32))
        ps_up = ctx.enter_context(nc.psum_tensor("ps_up", [P, 2, TOK], F32))
        ps_y = ctx.enter_context(nc.psum_tensor("ps_y", [P, CC, TOK], F32))
        ps_mix = ctx.enter_context(nc.psum_tensor("ps_mix", [P, CC, TOK], F32))
        ps_tok = ps_mix[:, :, :].rearrange("p c (n k) -> p (c n) k", k=CH)

        params_in = signal("params_in")
        w_in = [signal(f"w_in{i}") for i in range(STAGE)]
        w_hi_ready, w_lo_ready = signal("w_hi_ready"), signal("w_lo_ready")
        ident_zero, ident_ready, half_ready = signal("ident_zero"), signal("ident_ready"), signal("half_ready")
        dve_const, act_const, decay_exp, u_ready = (signal("dve_const"), signal("act_const"),
                                                    signal("decay_exp"), signal("u_ready"))
        xk_in, v_in, x_in = signal("xk_in", 16), signal("v_in", 16), signal("x_in", 16)
        k_bn, k_mv, k_eps, k_rs, k_norm = (signal("k_bn"), signal("k_mv"), signal("k_eps"),
                                          signal("k_rs"), signal("k_norm"))
        k_turned, e1_ready, e2_ready = signal("k_turned"), signal("e1_ready"), signal("e2_ready")
        ev_ready, ev2_ready, v0_kept = signal("ev_ready"), signal("ev2_ready"), signal("v0_kept")
        sum_a, sum_b, num_ready, den_ready = (signal("sum_a"), signal("sum_b"), signal("num_ready"),
                                              signal("den_ready"))
        rden_ready, y_ready, y0_ready, x1_new = (signal("rden_ready"), signal("y_ready"), signal("y0_ready"),
                                                 signal("x1_new"))
        x1_turned, h_bn, h_mv, h_eps, h_rs, h_norm = (signal("x1_turned"), signal("h_bn"), signal("h_mv"),
                                                     signal("h_eps"), signal("h_rs"), signal("h_norm"))
        h_turned, h_ready, logits_ready = signal("h_turned"), signal("h_ready"), signal("logits_ready")
        lmax_ready, lsub_ready, ex_ready = signal("lmax_ready"), signal("lsub_ready"), signal("ex_ready")
        esum_ready, rsum_ready, top_ready, top_cut = (signal("esum_ready"), signal("rsum_ready"),
                                                      signal("top_ready"), signal("top_cut"))
        rest_ready, cw_raw, cw_ready = signal("rest_ready"), signal("cw_raw"), signal("cw_ready")
        cw_turned, cw_copied, cw_stored = signal("cw_turned"), signal("cw_copied"), signal("cw_stored", 16)
        h_hi_ready, h_lo_ready, x1_kept = signal("h_hi_ready", CC), signal("h_lo_ready", CC), signal("x1_kept")
        gate_done, up_done, down_done = signal("gate_done", TILES), signal("up_done", TILES), signal("down_done", TILES)
        silu_ready, gu_ready, act_ready = signal("silu_ready", TILES), signal("gu_ready", TILES), signal("act_ready", TILES)
        a_hi_ready, a_lo_ready = signal("a_hi_ready", TILES), signal("a_lo_ready", TILES)
        cw_in = [signal(f"cw_in{i}", 16 * sum(len(owners(j)) for j in range(i, TILES, 2))) for i in range(2)]
        out_ready, stored = signal("out_ready"), signal("stored", 16)

        def cw_arrived(b, j):
            return cw_in[j % 2].at(b, 16 * sum(len(owners(i)) for i in range(j % 2, j + 1, 2)))

        block = ctx.enter_context(nc.Block())

        @block.sync
        def _(sp):
            def load_w(j):
                if j >= STAGE:
                    sp.wait_ge(w_lo_ready.sem, j - STAGE + 1)
                sp.dma_start(w_raw[:, j % STAGE, :], w_all[j]).then_inc(w_in[j % STAGE].sem, 16)

            def store_cw(b):
                sp.wait_ge(cw_copied.sem, cw_copied.at(b))
                sp.dma_start(cw_rows[bass.ds(b, 1), :, 0:width(b)].rearrange("a e t -> (a e) t"),
                             e2_den[0:EXPERTS, 0:width(b)]).then_inc(cw_stored.sem, 16)

            def spread_cw(b, j):
                n = b * TILES + j
                if j == 0:
                    sp.wait_ge(cw_stored.sem, cw_stored.at(b))
                if not (first(b) and j < 2):
                    sp.wait_ge(act_ready.sem, n - 1)
                for e, p0, p1 in owners(j):
                    row = cw_rows[bass.ds(b, 1), e, 0:width(b)]
                    sp.dma_start(cw_b[p0:p1, j % 2, 0:width(b)],
                                 row.broadcast_to([p1 - p0, width(b)])).then_inc(cw_in[j % 2].sem, 16)

            def store_result(b):
                sp.wait_ge(out_ready.sem, out_ready.at(b))
                sp.dma_start(out[:, :, bass.ds(b * MAIN, width(b))], chan(x1, b)).then_inc(stored.sem, 16)

            def tiles(b):
                for j in range(2, TILES):
                    spread_cw(b, j)
                    if first(b) and j - 2 + EARLY + STAGE < TILES:
                        load_w(j - 2 + EARLY + STAGE)

            def through(b):
                tiles(b)
                store_cw(b + 1)
                spread_cw(b + 1, 0)
                spread_cw(b + 1, 1)
                store_result(b)

            sp.dma_start(params[:, :, :], decay_u).then_inc(params_in.sem, 16)
            sp.dma_start(gw[:, :, :], gate_w).then_inc(params_in.sem, 16)
            sp.dma_start(g_raw[:, 0:1], gates[0:1].partition_broadcast(P)).then_inc(params_in.sem, 16)
            sp.dma_start(g_raw[:, 1:2], gates[1:2].partition_broadcast(P)).then_inc(params_in.sem, 16)
            for j in range(W_FIRST):
                load_w(j)
            store_cw(0)
            spread_cw(0, 0)
            spread_cw(0, 1)
            for j in range(W_FIRST, EARLY + STAGE):
                load_w(j)
            through(0)
            with sp.Fori(1, BLOCKS - 2) as b:
                through(b)
            through(BLOCKS - 2)
            tiles(BLOCKS - 1)
            store_result(BLOCKS - 1)
            sp.wait_ge(stored.sem, stored.at(BLOCKS - 1))

        @block.tensor
        def _(pe):
            def product(dst, pairs, start, stop):
                for i, ((s_hi, s_lo), (m_hi, m_lo)) in enumerate(pairs):
                    nc.tensor.matmul(dst, s_hi, m_hi, start=start and i == 0, stop=False)
                    nc.tensor.matmul(dst, s_hi, m_lo, start=False, stop=False)
                    last = nc.tensor.matmul(dst, s_lo, m_hi, start=False, stop=stop and i == len(pairs) - 1)
                return last

            def weights(j, part, c):
                cols = slice(part * CH + c * P, part * CH + (c + 1) * P)
                return w_hi[:, j, cols], w_lo[:, j, cols]

            def turn_k(b):
                pe.wait_ge(k_norm.sem, k_norm.at(b))
                if not first(b):
                    pe.wait_ge(cw_copied.sem, cw_copied.at(b - 1))
                for c in range(CC):
                    for n in range(width(b) // P):
                        mm = nc.tensor.transpose(ps_mix[:, c, n * P:(n + 1) * P], xk[:, n, c * P:(c + 1) * P],
                                                 ident[:, :])
                mm.then_inc(k_turned.sem, 1)

            def turn_x1(b):
                pe.wait_ge(x1_new.sem, x1_new.at(b))
                pe.wait_ge(e2_ready.sem, e2_ready.at(b))
                for n in range(width(b) // P):
                    for c in range(CC):
                        mm = nc.tensor.transpose(ps_tok[:, n, c * P:(c + 1) * P],
                                                 chan(x_x1, b)[:, c, n * P:(n + 1) * P], ident[:, :])
                mm.then_inc(x1_turned.sem, 1)

            def turn_h(b):
                pe.wait_ge(h_norm.sem, h_norm.at(b))
                for c in range(CC):
                    for n in range(width(b) // P):
                        mm = nc.tensor.transpose(ps_mix[:, c, n * P:(n + 1) * P],
                                                 tokm(e1_h, b)[:, n, c * P:(c + 1) * P], ident[:, :])
                mm.then_inc(h_turned.sem, 1)

            def logits(b):
                pe.wait_ge(h_ready.sem, h_ready.at(b))
                for n in range(width(b) // P):
                    for c in range(CC):
                        mm = nc.tensor.matmul(ps_mix[:, 1, n * EXPERTS:(n + 1) * EXPERTS],
                                              chan(b_h, b)[:, c, n * P:(n + 1) * P], gw[:, c, :],
                                              start=(c == 0), stop=(c == CC - 1))
                mm.then_inc(logits_ready.sem, 1)

            def turn_cw(b):
                pe.wait_ge(cw_ready.sem, cw_ready.at(b))
                for n in range(width(b) // P):
                    mm = nc.tensor.transpose(ps_mix[0:EXPERTS, 0, n * P:(n + 1) * P], cw[:, n, :], ident[:, :])
                mm.then_inc(cw_turned.sem, 1)

            def mix(b, slot):
                if slot == 4:
                    turn_k(b)
                if slot == 14:
                    turn_x1(b)
                if slot == 17:
                    turn_h(b)
                if slot == 18:
                    logits(b)
                if slot == 20:
                    turn_cw(b)

            def gate_up(b, j):
                n = b * TILES + j
                h = [(h_hi[:, c, 0:width(b)], h_lo[:, c, 0:width(b)]) for c in range(CC)]
                if first(b):
                    pe.wait_ge(w_lo_ready.sem, j + 1)
                if j == 0:
                    pe.wait_ge(h_lo_ready.sem, h_lo_ready.at(b))
                if not (first(b) and j < 2):
                    pe.wait_ge(silu_ready.sem, n - 1)
                product(ps_gate[:, j % 2, 0:width(b)], [(weights(j, 0, c), h[c]) for c in range(CC)],
                        True, True).then_inc(gate_done.sem, 1)
                if not (first(b) and j < 2):
                    pe.wait_ge(gu_ready.sem, n - 1)
                product(ps_up[:, j % 2, 0:width(b)], [(weights(j, 1, c), h[c]) for c in range(CC)],
                        True, True).then_inc(up_done.sem, 1)

            def down(b, j):
                n = b * TILES + j
                pe.wait_ge(a_lo_ready.sem, n + 1)
                if j == 0 and not first(b):
                    pe.wait_ge(out_ready.sem, out_ready.at(b - 1))
                a = (a_hi[:, j % 2, 0:width(b)], a_lo[:, j % 2, 0:width(b)])
                for c in range(CC):
                    mm = product(ps_y[:, c, 0:width(b)], [(weights(j, 2, c), a)], j == 0, j == TILES - 1)
                mm.then_inc(down_done.sem, 1)

            def tiles(b, ahead):
                for j in range(1, TILES):
                    gate_up(b, j)
                    if j >= 2:
                        down(b, j - 2)
                    if ahead:
                        mix(b + 1, j)
                down(b, TILES - 2)

            def through(b):
                tiles(b, True)
                gate_up(b + 1, 0)
                down(b, TILES - 1)

            pe.wait_ge(ident_ready.sem, 1)
            for slot in range(TILES):
                if slot == 18:
                    pe.wait_ge(params_in.sem, 64)
                if slot == 20:
                    gate_up(0, 0)
                mix(0, slot)
            through(0)
            with pe.Fori(1, BLOCKS - 2) as b:
                through(b)
            through(BLOCKS - 2)
            tiles(BLOCKS - 1, False)
            down(BLOCKS - 1, TILES - 1)

        @block.scalar
        def _(act):
            def load_xk(b):
                n = width(b) // STEPS
                act.dma_start(xk[:, 0:n, :], x_tok[:, bass.ds(b * (MAIN // STEPS), n), :]).then_inc(xk_in.sem, 16)

            def load_v(b):
                act.dma_start(chan(v_a, b), v_chan[:, :, bass.ds(b * MAIN, width(b))]).then_inc(v_in.sem, 16)

            def load_x(b):
                act.dma_start(chan(x_x1, b), x_chan[:, :, bass.ds(b * MAIN, width(b))]).then_inc(x_in.sem, 16)

            def split_w(j):
                act.wait_ge(w_in[j % STAGE].sem, 16 * (j // STAGE + 1))
                nc.scalar.copy(w_hi[:, j, :], w_raw[:, j % STAGE, :]).then_inc(w_hi_ready.sem, 1)

            def exps(b):
                act.wait_ge(k_turned.sem, k_turned.at(b))
                nc.scalar.activation(chan(e1_h, b), ps_mix[:, :, 0:width(b)], ACT.Exp).then_inc(e1_ready.sem, 1)
                if not first(b):
                    act.wait_ge(cw_stored.sem, cw_stored.at(b - 1))
                for c in range(CC):
                    last = nc.scalar.activation(chan(e2_den, b)[:, c, :], ps_mix[:, c, 0:width(b)], ACT.Exp,
                                                bias=u_min[:, c:c + 1])
                last.then_inc(e2_ready.sem, 1)

            def mix(b, slot):
                if slot == 1:
                    if not first(b):
                        act.wait_ge(x1_new.sem, x1_new.at(b - 1))
                    load_xk(b)
                    load_v(b)
                if slot == 4:
                    exps(b)
                if slot == 17:
                    act.wait_ge(h_turned.sem, h_turned.at(b))
                    nc.scalar.copy(chan(b_h, b), ps_mix[:, :, 0:width(b)]).then_inc(h_ready.sem, 1)
                if slot == 18:
                    n = width(b) // STEPS
                    act.wait_ge(lsub_ready.sem, lsub_ready.at(b))
                    nc.scalar.activation(ex[:, 0:n, 0:EXPERTS], lsub[:, 0:n, :], ACT.Exp).then_inc(ex_ready.sem, 1)
                if slot == 20:
                    act.wait_ge(cw_turned.sem, cw_turned.at(b))
                    nc.scalar.copy(e2_den[0:EXPERTS, 0:width(b)],
                                   ps_mix[0:EXPERTS, 0, 0:width(b)]).then_inc(cw_copied.sem, 1)

            def split_h(b):
                if not first(b):
                    act.wait_ge(up_done.sem, up_done.at(b - 1))
                act.wait_ge(h_ready.sem, h_ready.at(b))
                for c in range(CC):
                    nc.scalar.copy(h_hi[:, c, 0:width(b)], chan(b_h, b)[:, c, :]).then_inc(h_hi_ready.sem, 1)

            def keep_x1(b):
                if not first(b):
                    act.wait_ge(stored.sem, stored.at(b - 1))
                act.wait_ge(x1_turned.sem, x1_turned.at(b))
                nc.scalar.copy(flat(x1, b), flat(x_x1, b)).then_inc(x1_kept.sem, 1)

            def tile(b, j):
                n = b * TILES + j
                act.wait_ge(gate_done.sem, n + 1)
                if not (first(b) and j < 2):
                    act.wait_ge(a_lo_ready.sem, n - 1)
                nc.scalar.activation(a32[:, j % 2, 0:width(b)], ps_gate[:, j % 2, 0:width(b)],
                                     ACT.Silu).then_inc(silu_ready.sem, 1)
                if first(b) and j + EARLY < TILES:
                    split_w(j + EARLY)
                if j == TILES - 1 and not (isinstance(b, int) and b == BLOCKS - 1):
                    split_h(b + 1)
                act.wait_ge(act_ready.sem, n + 1)
                if not (first(b) and j < 2):
                    act.wait_ge(down_done.sem, n - 1)
                nc.scalar.copy(a_hi[:, j % 2, 0:width(b)], a32[:, j % 2, 0:width(b)]).then_inc(a_hi_ready.sem, 1)

            def tiles(b, ahead):
                for j in range(1, TILES):
                    tile(b, j)
                    if ahead:
                        mix(b + 1, j)
                    if j == 5:
                        keep_x1(b)
                        if ahead:
                            act.wait_ge(x1_kept.sem, x1_kept.at(b))
                            load_x(b + 1)

            def through(b):
                tiles(b, True)
                tile(b + 1, 0)

            mix(0, 1)
            load_x(0)
            act.wait_ge(params_in.sem, 64)
            nc.scalar.activation(g_tanh[:, :], g_raw[:, :], ACT.Tanh).then_inc(act_const.sem, 1)
            nc.scalar.activation(decay_col[:, 0, :], params[:, 0, :], ACT.Exp).then_inc(decay_exp.sem, 1)
            act.wait_ge(decay_exp.sem, 1)
            nc.scalar.activation(decay_col[:, 1, :], decay_col[:, 0, :], ACT.Exp, scale=-1.0).then_inc(act_const.sem, 1)
            act.wait_ge(u_ready.sem, 2)
            nc.scalar.activation(c1[:, :], u_max[:, :], ACT.Exp, scale=-1.0).then_inc(act_const.sem, 1)
            early = {4: range(0, 7), 17: range(7, 8), 18: range(8, EARLY)}
            for slot in range(2, TILES):
                mix(0, slot)
                if slot == 17:
                    split_h(0)
                for j in early.get(slot, ()):
                    split_w(j)
            tile(0, 0)
            through(0)
            with act.Fori(1, BLOCKS - 2) as b:
                through(b)
            through(BLOCKS - 2)
            tiles(BLOCKS - 1, False)

        @block.gpsimd
        def _(pool):
            def split_w(j):
                pool.wait_ge(w_hi_ready.sem, j + 1)
                nc.gpsimd.tensor_tensor(w_lo[:, j, :], w_raw[:, j % STAGE, :], w_hi[:, j, :].bitcast(F32),
                                        ALU.subtract).then_inc(w_lo_ready.sem, 1)

            def inverse_deviation(b, eps_done, rs_done):
                n = width(b) // STEPS
                pool.wait_ge(eps_done.sem, eps_done.at(b))
                nc.gpsimd.tensor_tensor(rs[:, 0:n], var_eps[:, 0:n], minus_half[:, 0:n], ALU.pow).then_inc(rs_done.sem, 1)

            def weigh_v_new(b):
                pool.wait_ge(v_in.sem, v_in.at(b))
                pool.wait_ge(e2_ready.sem, e2_ready.at(b))
                if not first(b):
                    pool.wait_ge(x1_new.sem, x1_new.at(b - 1))
                nc.gpsimd.tensor_tensor(flat(num_y, b), flat(e2_den, b), flat(v_a, b), ALU.mult).then_inc(ev2_ready.sem, 1)

            def weigh_v(b):
                pool.wait_ge(e1_ready.sem, e1_ready.at(b))
                pool.wait_ge(ev2_ready.sem, ev2_ready.at(b))
                pool.wait_ge(v0_kept.sem, v0_kept.at(b))
                nc.gpsimd.tensor_tensor(flat(v_a, b), flat(e1_h, b), flat(v_a, b), ALU.mult).then_inc(ev_ready.sem, 1)

            def tile(b, j):
                n = b * TILES + j
                pool.wait_ge(a_hi_ready.sem, n + 1)
                nc.gpsimd.tensor_tensor(a_lo[:, j % 2, 0:width(b)], a32[:, j % 2, 0:width(b)],
                                        a_hi[:, j % 2, 0:width(b)].bitcast(F32),
                                        ALU.subtract).then_inc(a_lo_ready.sem, 1)
                if first(b) and j + EARLY < TILES:
                    split_w(j + EARLY)

            def tiles(b, ahead):
                for j in range(1, TILES):
                    if ahead and j == 5:
                        weigh_v_new(b + 1)
                    if ahead and j == 7:
                        weigh_v(b + 1)
                    tile(b, j)
                    if ahead and j == 2:
                        inverse_deviation(b + 1, k_eps, k_rs)
                    if ahead and j == 15:
                        inverse_deviation(b + 1, h_eps, h_rs)

            def through(b):
                tiles(b, True)
                tile(b + 1, 0)

            nc.gpsimd.memset(ident[:, :], 0.0).then_inc(ident_zero.sem, 1)
            pool.wait_ge(ident_zero.sem, 1)
            nc.gpsimd.affine_select(out=ident[:, :], in_=ident[:, :], compare_op=ALU.not_equal, fill=1.0, base=0,
                                    pattern=[[-1, P]], channel_multiplier=1).then_inc(ident_ready.sem, 1)
            nc.gpsimd.memset(minus_half[:, :], -0.5).then_inc(half_ready.sem, 1)
            pool.wait_ge(half_ready.sem, 1)
            inverse_deviation(0, k_eps, k_rs)
            weigh_v_new(0)
            weigh_v(0)
            for j in range(EARLY_LN):
                split_w(j)
            inverse_deviation(0, h_eps, h_rs)
            for j in range(EARLY_LN, EARLY):
                split_w(j)
            tile(0, 0)
            through(0)
            with pool.Fori(1, BLOCKS - 2) as b:
                through(b)
            through(BLOCKS - 2)
            tiles(BLOCKS - 1, False)

        @block.vector
        def _(dve):
            def statistics(b, src, bn_done, mv_done, eps_done):
                n = width(b) // STEPS
                for i in range(n):
                    last = nc.vector.bn_stats(bn[:, i, :], src[:, i, :])
                last.then_inc(bn_done.sem, 1)
                dve.wait_ge(bn_done.sem, bn_done.at(b))
                nc.vector.memset(carrier[:, :], 0.0)
                for i in range(n):
                    last = nc.vector.bn_aggr(mv[:, i, :], bn[:, i, :])
                last.then_inc(mv_done.sem, 1)
                dve.wait_ge(mv_done.sem, mv_done.at(b))
                nc.vector.tensor_scalar(var_eps[:, 0:n], mv[:, 0:n, 1], EPS, None, ALU.add).then_inc(eps_done.sem, 1)

            def normalise(b, dst, src, rs_done, norm_done):
                n = width(b) // STEPS
                dve.wait_ge(rs_done.sem, rs_done.at(b))
                for i in range(n):
                    last = nc.vector.tensor_scalar(dst[:, i, :], src[:, i, :], mv[:, i, 0:1], rs[:, i:i + 1],
                                                   ALU.subtract, ALU.mult)
                last.then_inc(norm_done.sem, 1)

            def decayed_sums(b, dst, src, done):
                nc.vector.tensor_tensor_scan(flat(dst, b), decay[:, TOK - width(b):TOK + width(b)], flat(src, b),
                                             0.0, ALU.mult, ALU.add).then_inc(done.sem, 1)

            def add_sums(b, dst, sums, done):
                n = width(b) // STEPS
                for c in range(CC):
                    s = slice(c * n, (c + 1) * n)
                    last = nc.vector.scalar_tensor_tensor(seqs(dst, b)[:, s, 1:STEPS], seqs(sums, b)[:, s, 0:STEPS - 1],
                                                          c1[:, c:c + 1], seqs(dst, b)[:, s, 1:STEPS], ALU.mult, ALU.add)
                last.then_inc(done.sem, 1)

            def route(b):
                n = width(b) // STEPS
                dve.wait_ge(ex_ready.sem, ex_ready.at(b))
                nc.vector.tensor_reduce(esum[:, 0:n], ex[:, 0:n, 0:EXPERTS], AX.X, ALU.add).then_inc(esum_ready.sem, 1)
                for i in range(n):
                    last = nc.vector.max(top[:, i, :], ex[:, i, :])
                last.then_inc(top_ready.sem, 1)
                dve.wait_ge(top_ready.sem, top_ready.at(b))
                nc.vector.memset(top[:, 0:n, TOPK:8], -1.0).then_inc(top_cut.sem, 1)
                dve.wait_ge(top_cut.sem, top_cut.at(b))
                dve.wait_ge(esum_ready.sem, esum_ready.at(b))
                nc.vector.reciprocal(rsum[:, 0:n], esum[:, 0:n]).then_inc(rsum_ready.sem, 1)
                for i in range(n):
                    last = nc.vector.match_replace(rest[:, i, :], top[:, i, :], ex[:, i, :], 0.0)
                last.then_inc(rest_ready.sem, 1)
                dve.wait_ge(rest_ready.sem, rest_ready.at(b))
                nc.vector.tensor_tensor(cw[:, 0:n, :], ex[:, 0:n, 0:EXPERTS], rest[:, 0:n, 0:EXPERTS],
                                        ALU.subtract).then_inc(cw_raw.sem, 1)
                dve.wait_ge(cw_raw.sem, cw_raw.at(b))
                dve.wait_ge(rsum_ready.sem, rsum_ready.at(b))
                nc.vector.tensor_tensor(cw[:, 0:n, :], cw[:, 0:n, :],
                                        rsum[:, 0:n].unsqueeze(2).to_broadcast([P, n, EXPERTS]),
                                        ALU.mult).then_inc(cw_ready.sem, 1)

            def mix(b, slot):
                n = width(b) // STEPS
                if slot == 2:
                    dve.wait_ge(xk_in.sem, xk_in.at(b))
                    statistics(b, xk, k_bn, k_mv, k_eps)
                if slot == 3:
                    normalise(b, xk, xk, k_rs, k_norm)
                if slot == 5:
                    dve.wait_ge(v_in.sem, v_in.at(b))
                    nc.vector.tensor_copy(v0[:, 0:CC * n], seqs(v_a, b)[:, :, 0]).then_inc(v0_kept.sem, 1)
                    dve.wait_ge(e1_ready.sem, e1_ready.at(b))
                    decayed_sums(b, b_h, e1_h, sum_b)
                if slot == 7:
                    dve.wait_ge(sum_b.sem, sum_b.at(b))
                    dve.wait_ge(ev2_ready.sem, ev2_ready.at(b))
                    add_sums(b, e2_den, b_h, den_ready)
                if 7 <= slot < 7 + RECIPS:
                    if slot == 7:
                        dve.wait_ge(den_ready.sem, den_ready.at(b))
                    s = slice(CC * n * (slot - 7) // RECIPS, CC * n * (slot - 6) // RECIPS)
                    ins = nc.vector.reciprocal(seqs(e2_den, b)[:, s, 1:STEPS], seqs(e2_den, b)[:, s, 1:STEPS])
                    if slot == 6 + RECIPS:
                        ins.then_inc(rden_ready.sem, 1)
                if slot == 11:
                    dve.wait_ge(ev_ready.sem, ev_ready.at(b))
                    decayed_sums(b, v_a, v_a, sum_a)
                    dve.wait_ge(sum_a.sem, sum_a.at(b))
                    add_sums(b, num_y, v_a, num_ready)
                if slot == 12:
                    dve.wait_ge(rden_ready.sem, rden_ready.at(b))
                    dve.wait_ge(num_ready.sem, num_ready.at(b))
                    nc.vector.tensor_tensor(seqs(num_y, b)[:, :, 1:STEPS], seqs(num_y, b)[:, :, 1:STEPS],
                                            seqs(e2_den, b)[:, :, 1:STEPS], ALU.mult).then_inc(y_ready.sem, 1)
                    nc.vector.tensor_copy(seqs(num_y, b)[:, :, 0], v0[:, 0:CC * n]).then_inc(y0_ready.sem, 1)
                if slot == 13:
                    dve.wait_ge(y_ready.sem, y_ready.at(b))
                    dve.wait_ge(y0_ready.sem, y0_ready.at(b))
                    dve.wait_ge(x_in.sem, x_in.at(b))
                    nc.vector.scalar_tensor_tensor(flat(x_x1, b), flat(num_y, b), g_tanh[:, 0:1], flat(x_x1, b),
                                                   ALU.mult, ALU.add).then_inc(x1_new.sem, 1)
                if slot == 15:
                    dve.wait_ge(x1_turned.sem, x1_turned.at(b))
                    statistics(b, ps_tok, h_bn, h_mv, h_eps)
                if slot == 16:
                    normalise(b, tokm(e1_h, b), ps_tok, h_rs, h_norm)
                if slot == 18:
                    dve.wait_ge(logits_ready.sem, logits_ready.at(b))
                    rows = ps_mix[:, 1, 0:n * EXPERTS].rearrange("p (n e) -> p n e", n=n)
                    nc.vector.tensor_reduce(lmax[:, 0:n], rows, AX.X, ALU.max).then_inc(lmax_ready.sem, 1)
                    dve.wait_ge(lmax_ready.sem, lmax_ready.at(b))
                    nc.vector.tensor_tensor(lsub[:, 0:n, :], rows,
                                            lmax[:, 0:n].unsqueeze(2).to_broadcast([P, n, EXPERTS]),
                                            ALU.subtract).then_inc(lsub_ready.sem, 1)
                if slot == 19:
                    route(b)

            def split_h(b):
                for c in range(CC):
                    dve.wait_ge(h_hi_ready.sem, h_hi_ready.at(b, c + 1))
                    nc.vector.tensor_tensor(h_lo[:, c, 0:width(b)], chan(b_h, b)[:, c, :],
                                            h_hi[:, c, 0:width(b)].bitcast(F32),
                                            ALU.subtract).then_inc(h_lo_ready.sem, 1)

            def result(b):
                dve.wait_ge(down_done.sem, down_done.at(b))
                dve.wait_ge(x1_kept.sem, x1_kept.at(b))
                nc.vector.scalar_tensor_tensor(chan(x1, b), ps_y[:, :, 0:width(b)], g_tanh[:, 1:2], chan(x1, b),
                                               ALU.mult, ALU.add).then_inc(out_ready.sem, 1)

            def tile(b, j):
                n = b * TILES + j
                a = a32[:, j % 2, 0:width(b)]
                dve.wait_ge(silu_ready.sem, n + 1)
                dve.wait_ge(up_done.sem, n + 1)
                nc.vector.tensor_tensor(a, a, ps_up[:, j % 2, 0:width(b)], ALU.mult).then_inc(gu_ready.sem, 1)
                dve.wait_ge(gu_ready.sem, n + 1)
                dve.wait_ge(cw_in[j % 2].sem, cw_arrived(b, j))
                nc.vector.tensor_tensor(a, a, cw_b[:, j % 2, 0:width(b)], ALU.mult).then_inc(act_ready.sem, 1)

            def tiles(b, ahead):
                for j in range(1, TILES):
                    tile(b, j)
                    if ahead:
                        mix(b + 1, j)
                if ahead:
                    split_h(b + 1)

            def through(b):
                tiles(b, True)
                tile(b + 1, 0)
                result(b)

            nc.vector.memset(decay[:, :], 0.0).then_inc(dve_const.sem, 1)
            nc.vector.memset(ex[:, :, EXPERTS:PAD], -1.0).then_inc(dve_const.sem, 1)
            dve.wait_ge(params_in.sem, 64)
            nc.vector.tensor_scalar(u_min[:, :], params[:, 1, :], 0.0, None, ALU.min).then_inc(u_ready.sem, 1)
            nc.vector.tensor_scalar(u_max[:, :], params[:, 1, :], 0.0, None, ALU.max).then_inc(u_ready.sem, 1)
            mix(0, 2)
            mix(0, 3)
            dve.wait_ge(act_const.sem, 3)
            dve.wait_ge(dve_const.sem, 2)
            for c in range(CC):
                part = decay[:, c * TOK:(c + 1) * TOK].rearrange("p (s t) -> p s t", t=STEPS)[:, :, 1:STEPS]
                nc.vector.tensor_scalar(part, part, decay_col[:, 1, c:c + 1], None, ALU.add).then_inc(dve_const.sem, 1)
            dve.wait_ge(dve_const.sem, 2 + CC)
            for slot in range(4, TILES):
                mix(0, slot)
                if slot == 17:
                    split_h(0)
            tile(0, 0)
            through(0)
            with dve.Fori(1, BLOCKS - 2) as b:
                through(b)
            through(BLOCKS - 2)
            tiles(BLOCKS - 1, False)
            result(BLOCKS - 1)


def kernel(x, ctx_2048, g_xattn, g_ffn, L0_xattn_time_decay, L0_xattn_time_first,
           L0_ffn_gate_w, L0_ffn_w_gate, L0_ffn_w_up, L0_ffn_w_down):
    import numpy as np
    import concourse.bacc as bacc
    from concourse.bass_utils import run_bass_kernel_spmd

    def chan_major(a):
        return np.ascontiguousarray(np.asarray(a).reshape(TOKENS, CC, P).transpose(2, 1, 0))

    def row_tiles(a):
        return a.reshape(TILES, P, CC, P).transpose(0, 3, 2, 1).reshape(TILES, P, CH)

    w_gate, w_up, w_down = np.asarray(L0_ffn_w_gate), np.asarray(L0_ffn_w_up), np.asarray(L0_ffn_w_down)
    arrays = {
        "x_tok": np.ascontiguousarray(np.asarray(x).transpose(1, 0, 2)),
        "x_chan": chan_major(x),
        "v_chan": chan_major(ctx_2048),
        "w_all": np.ascontiguousarray(np.concatenate(
            [row_tiles(w_gate), row_tiles(w_up), w_down.transpose(0, 2, 1).reshape(TILES, P, CH)], axis=2)),
        "gate_w": np.ascontiguousarray(np.asarray(L0_ffn_gate_w).reshape(EXPERTS, CC, P).transpose(2, 1, 0)),
        "decay_u": np.ascontiguousarray(np.stack(
            [np.asarray(L0_xattn_time_decay), np.asarray(L0_xattn_time_first)]).reshape(2, CC, P).transpose(2, 0, 1)),
        "gates": np.concatenate([np.asarray(g_xattn), np.asarray(g_ffn)]),
    }
    nc = bacc.Bacc("TRN2", target_bir_lowering=False, num_devices=1)
    args = [nc.dram_tensor(name, a.shape, mybir.dt.from_np(a.dtype), kind="ExternalInput").ap()
            for name, a in arrays.items()]
    out = nc.dram_tensor("out", (P, CC, TOKENS), F32, kind="ExternalOutput").ap()
    program(nc, *args, out)
    r = run_bass_kernel_spmd(nc, [arrays], core_ids=[0])
    return np.ascontiguousarray(r.results[0]["out"].transpose(2, 1, 0)).reshape(SEQS, STEPS, CH)
```

```python
from contextlib import ExitStack

import concourse.bass as bass
from concourse import mybir

F32 = mybir.dt.float32
F32R = mybir.dt.float32r
ALU = mybir.AluOpType
ACT = mybir.ActivationFunctionType
AX = mybir.AxisListType

P = 128
SEQS, STEPS, CH = 16, 128, 256
EXPERTS, FEAT, TOPK = 16, 176, 6
CC = CH // P
TOKENS = SEQS * STEPS
MAIN = 384
TOK = 512
BLOCKS = (TOKENS - TOK) // MAIN + 1
TILES = EXPERTS * FEAT // P
WCOLS = 3 * CH
STAGE = 4
PAD = EXPERTS + 2
EPS = 1e-5
EARLY = 9
EARLY_LN = 3
DVE_SPLITS = (10, 11, 13, 14)
EXP_SLOTS = (3, 18)
RECIPS = 6


def owners(j):
    f0, f1 = j * P, (j + 1) * P
    return [(e, max(f0, e * FEAT) - f0, min(f1, (e + 1) * FEAT) - f0) for e in range(f0 // FEAT, (f1 - 1) // FEAT + 1)]


class Signal:

    def __init__(self, sem, per):
        self.sem, self.per = sem, per

    def at(self, b, k=None):
        return b * self.per + (self.per if k is None else k)


class SeqSignal(Signal):

    def __init__(self, sem):
        super().__init__(sem, MAIN // STEPS)

    def at(self, b, k=None):
        return b * self.per + (width(b) // STEPS if k is None else k)


def bank_mates(b, i):
    return min(width(b) // STEPS, i // 2 * 2 + 2)


def first(b):
    return isinstance(b, int) and b == 0


def width(b):
    return TOK if isinstance(b, int) and b == BLOCKS - 1 else MAIN


def program(nc, x_tok, x_chan, v_chan, w_all, gate_w, decay_u, gates, out):
    cw_rows = nc.dram_tensor("cw_rows", (BLOCKS, EXPERTS, TOK), F32, kind="Internal").ap()

    with ExitStack() as ctx:
        def sb(name, shape, dt=F32):
            return ctx.enter_context(nc.sbuf_tensor(name, shape, dt))

        def signal(name, per=1):
            return Signal(ctx.enter_context(nc.semaphore(name)), per)

        def seq_signal(name):
            return SeqSignal(ctx.enter_context(nc.semaphore(name)))

        w_hi = sb("w_hi", [P, TILES, WCOLS], F32R)
        w_lo = sb("w_lo", [P, TILES, WCOLS], F32R)
        w_raw = sb("w_raw", [P, STAGE, WCOLS])
        xk = sb("xk", [P, TOK // STEPS, CH])
        v_a = sb("v_a", [P, CC * TOK])
        x_x1 = sb("x_x1", [P, CC * TOK])
        e1_h = sb("e1_h", [P, CC * TOK])
        b_h = sb("b_h", [P, CC * TOK])
        e2_den = sb("e2_den", [P, CC * TOK])
        num_y = sb("num_y", [P, CC * TOK])
        decay = sb("decay", [P, CC * TOK])
        x1 = sb("x1", [P, CC * TOK])
        h_hi = sb("h_hi", [P, CC, TOK], F32R)
        h_lo = sb("h_lo", [P, CC, TOK], F32R)
        cw_b = sb("cw_b", [P, 2, TOK])
        a32 = sb("a32", [P, 2, TOK])
        a_hi = sb("a_hi", [P, 2, TOK], F32R)
        a_lo = sb("a_lo", [P, 2, TOK], F32R)
        ident = sb("ident", [P, P])
        gw = sb("gw", [P, CC, EXPERTS])
        params = sb("params", [P, 2, CC])
        g_raw = sb("g_raw", [P, 2])
        g_tanh = sb("g_tanh", [P, 2])
        decay_col = sb("decay_col", [P, 2, CC])
        u_min = sb("u_min", [P, CC])
        minus_u = sb("minus_u", [P, CC])
        minus_half = sb("minus_half", [P, TOK // STEPS])
        carrier = sb("carrier", [P, 1])
        v0 = sb("v0", [P, CC * TOK // STEPS])
        bn = sb("bn", [P, TOK // STEPS, 6])
        mv = sb("mv", [P, TOK // STEPS, 2])
        var_eps = sb("var_eps", [P, TOK // STEPS])
        rs = sb("rs", [P, TOK // STEPS])
        lmax = sb("lmax", [P, TOK // STEPS])
        lsub = sb("lsub", [P, TOK // STEPS, EXPERTS])
        ex = sb("ex", [P, TOK // STEPS, PAD])
        esum = sb("esum", [P, TOK // STEPS])
        rsum = sb("rsum", [P, TOK // STEPS])
        top = sb("top", [P, TOK // STEPS, 8])
        rest = sb("rest", [P, TOK // STEPS, PAD])
        cw = sb("cw", [P, TOK // STEPS, EXPERTS])

        def chan(buf, b):
            return buf[:, 0:CC * width(b)].rearrange("p (c t) -> p c t", c=CC)

        def seqs(buf, b):
            return buf[:, 0:CC * width(b)].rearrange("p (s t) -> p s t", t=STEPS)

        def flat(buf, b):
            return buf[:, 0:CC * width(b)]

        def tokm(buf, b):
            return buf[:, 0:CC * width(b)].rearrange("p (n c) -> p n c", c=CH)

        def den(b):
            return x1 if first(b) else e2_den

        ps_gate = ctx.enter_context(nc.psum_tensor("ps_gate", [P, 2, TOK], F32))
        ps_up = ctx.enter_context(nc.psum_tensor("ps_up", [P, 2, TOK], F32))
        ps_y = ctx.enter_context(nc.psum_tensor("ps_y", [P, CC, TOK], F32))
        ps_mix = ctx.enter_context(nc.psum_tensor("ps_mix", [P, CC, TOK], F32))
        ps_tok = ps_mix[:, :, :].rearrange("p c (n k) -> p (c n) k", k=CH)

        params_in = signal("params_in")
        w_in = [signal(f"w_in{i}") for i in range(STAGE)]
        w_hi_ready = signal("w_hi_ready")
        w_lo_pool, w_lo_dve = signal("w_lo_pool"), signal("w_lo_dve")
        ident_zero, ident_ready, half_ready = signal("ident_zero"), signal("ident_ready"), signal("half_ready")
        dve_const, act_const, decay_exp, u_ready = (signal("dve_const"), signal("act_const"),
                                                    signal("decay_exp"), signal("u_ready"))
        xk_in, v_in, x_in = signal("xk_in", 16), signal("v_in", 16), signal("x_in", 16)
        k_bn, k_mv, k_eps, k_rs, k_norm = (signal("k_bn"), signal("k_mv"), signal("k_eps"),
                                          signal("k_rs"), seq_signal("k_norm"))
        k_turned, e1_ready, e2_ready = signal("k_turned"), signal("e1_ready"), signal("e2_ready")
        ev_ready, ev2_ready, v0_kept = signal("ev_ready"), signal("ev2_ready"), signal("v0_kept")
        sum_a, sum_b, num_ready, den_ready = (signal("sum_a"), signal("sum_b"), signal("num_ready"),
                                              signal("den_ready"))
        rden_ready, y_ready, y0_ready, x1_new = (seq_signal("rden_ready"), seq_signal("y_ready"), signal("y0_ready"),
                                                 seq_signal("x1_new"))
        x1_turned, h_bn, h_mv, h_eps, h_rs, h_norm = (seq_signal("x1_turned"), signal("h_bn"), signal("h_mv"),
                                                     signal("h_eps"), signal("h_rs"), seq_signal("h_norm"))
        h_turned, h_ready, logits_ready = seq_signal("h_turned"), seq_signal("h_ready"), signal("logits_ready")
        lmax_ready, lsub_ready, ex_ready = signal("lmax_ready"), signal("lsub_ready"), signal("ex_ready")
        esum_ready, rsum_ready, top_ready, top_cut = (signal("esum_ready"), signal("rsum_ready"),
                                                      signal("top_ready"), signal("top_cut"))
        rest_ready, cw_raw, cw_ready = signal("rest_ready"), signal("cw_raw"), signal("cw_ready")
        cw_spread = signal("cw_spread")
        cw_turned, cw_copied, cw_stored = signal("cw_turned"), signal("cw_copied"), signal("cw_stored", 16)
        h_hi_ready, h_lo_ready, x1_kept = signal("h_hi_ready", CC), signal("h_lo_ready", CC), signal("x1_kept")
        gate_done, up_done, down_done = signal("gate_done", TILES), signal("up_done", TILES), signal("down_done", TILES)
        silu_ready, gu_ready, act_ready = (signal("silu_ready", TILES), signal("gu_ready", TILES),
                                           signal("act_ready", TILES))
        a_hi_ready, a_lo_ready = signal("a_hi_ready", TILES), signal("a_lo_ready", TILES)
        cw_in = [signal(f"cw_in{i}", 16 * sum(len(owners(j)) for j in range(i, TILES, 2))) for i in range(2)]
        sum0_ready = signal("sum0_ready")
        out_ready, stored = signal("out_ready", CC), signal("stored", 16 * CC)

        def wait_w_lo(engine, j):
            if j in DVE_SPLITS:
                engine.wait_ge(w_lo_dve.sem, sum(i <= j for i in DVE_SPLITS))
            else:
                engine.wait_ge(w_lo_pool.sem, j + 1 - sum(i < j for i in DVE_SPLITS))

        def cw_arrived(b, j):
            rows = sum(len(owners(i)) for i in range(j % 2, j + 1, 2)) - len(owners(j % 2))
            return cw_in[j % 2].at(b, 16 * rows)

        def add_sums(engine, b, dst, new, sums, done):
            engine.tensor_tensor(seqs(dst, b)[:, :, 1:STEPS], seqs(sums, b)[:, :, 0:STEPS - 1],
                                 seqs(new, b)[:, :, 1:STEPS], ALU.add).then_inc(done.sem, 1)

        def numerator(engine, b):
            engine.wait_ge(ev2_ready.sem, ev2_ready.at(b))
            engine.wait_ge(sum_a.sem, sum_a.at(b))
            add_sums(engine, b, num_y, num_y, v_a, num_ready)

        def quotient(engine, b, i):
            later = slice(i * STEPS + 1, (i + 1) * STEPS)
            engine.wait_ge(rden_ready.sem, rden_ready.at(b, i + 1))
            engine.wait_ge(num_ready.sem, num_ready.at(b))
            engine.tensor_tensor(chan(num_y, b)[:, :, later], chan(num_y, b)[:, :, later],
                                 chan(den(b), b)[:, :, later], ALU.mult).then_inc(y_ready.sem, 1)

        block = ctx.enter_context(nc.Block())

        @block.sync
        def _(sp):
            def load_w(j):
                if j >= STAGE:
                    wait_w_lo(sp, j - STAGE)
                sp.dma_start(w_raw[:, j % STAGE, :], w_all[j]).then_inc(w_in[j % STAGE].sem, 16)

            def store_cw(b):
                sp.wait_ge(cw_copied.sem, cw_copied.at(b))
                sp.dma_start(cw_rows[bass.ds(b, 1), :, 0:width(b)].rearrange("a e t -> (a e) t"),
                             e2_den[0:EXPERTS, 0:width(b)]).then_inc(cw_stored.sem, 16)

            def spread_cw(b, j):
                n = b * TILES + j
                if j == (2 if first(b) else 0):
                    sp.wait_ge(cw_stored.sem, cw_stored.at(b))
                if not (first(b) and j < 2):
                    sp.wait_ge(act_ready.sem, n - 1)
                for e, p0, p1 in owners(j):
                    row = cw_rows[bass.ds(b, 1), e, 0:width(b)]
                    sp.dma_start(cw_b[p0:p1, j % 2, 0:width(b)],
                                 row.broadcast_to([p1 - p0, width(b)])).then_inc(cw_in[j % 2].sem, 16)

            def store_result(b):
                for c in range(CC):
                    sp.wait_ge(out_ready.sem, out_ready.at(b, c + 1))
                    sp.dma_start(out[:, c, bass.ds(b * MAIN, width(b))], chan(x1, b)[:, c, :]).then_inc(stored.sem, 16)

            def tiles(b):
                for j in range(2, TILES):
                    spread_cw(b, j)
                    if first(b) and j - 2 + EARLY + STAGE < TILES:
                        load_w(j - 2 + EARLY + STAGE)

            def through(b):
                tiles(b)
                store_cw(b + 1)
                spread_cw(b + 1, 0)
                spread_cw(b + 1, 1)
                store_result(b)

            sp.dma_start(params[:, :, :], decay_u).then_inc(params_in.sem, 16)
            sp.dma_start(gw[:, :, :], gate_w).then_inc(params_in.sem, 16)
            sp.dma_start(g_raw[:, 0:1], gates[0:1].partition_broadcast(P)).then_inc(params_in.sem, 16)
            sp.dma_start(g_raw[:, 1:2], gates[1:2].partition_broadcast(P)).then_inc(params_in.sem, 16)
            for j in range(EARLY + STAGE):
                load_w(j)
            store_cw(0)
            through(0)
            with sp.Fori(1, BLOCKS - 2) as b:
                through(b)
            through(BLOCKS - 2)
            tiles(BLOCKS - 1)
            store_result(BLOCKS - 1)
            sp.wait_ge(stored.sem, stored.at(BLOCKS - 1))

        @block.tensor
        def _(pe):
            def times_hi(dst, w, m_hi, start):
                nc.tensor.matmul(dst, w[0], m_hi, start=start, stop=False)
                nc.tensor.matmul(dst, w[1], m_hi, start=False, stop=False)

            def times_lo(dst, w, m_lo, stop):
                return nc.tensor.matmul(dst, w[0], m_lo, start=False, stop=stop)

            def weights(j, part, c):
                cols = slice(part * CH + c * P, part * CH + (c + 1) * P)
                return w_hi[:, j, cols], w_lo[:, j, cols]

            def turn_k(b):
                if not first(b):
                    pe.wait_ge(cw_copied.sem, cw_copied.at(b - 1))
                for n in range(width(b) // P):
                    pe.wait_ge(k_norm.sem, k_norm.at(b, n + 1))
                    for c in range(CC):
                        mm = nc.tensor.transpose(ps_mix[:, c, n * P:(n + 1) * P], xk[:, n, c * P:(c + 1) * P],
                                                 ident[:, :])
                mm.then_inc(k_turned.sem, 1)

            def turn_x1(b):
                pe.wait_ge(e2_ready.sem, e2_ready.at(b))
                for n in range(width(b) // P):
                    pe.wait_ge(x1_new.sem, x1_new.at(b, n + 1))
                    for c in range(CC):
                        mm = nc.tensor.transpose(ps_tok[:, n, c * P:(c + 1) * P],
                                                 chan(x_x1, b)[:, c, n * P:(n + 1) * P], ident[:, :])
                    mm.then_inc(x1_turned.sem, 1)

            def turn_h(b):
                for n in range(width(b) // P):
                    pe.wait_ge(h_norm.sem, h_norm.at(b, bank_mates(b, n)))
                    for c in range(CC):
                        mm = nc.tensor.transpose(ps_tok[:, n, c * P:(c + 1) * P],
                                                 tokm(e1_h, b)[:, n, c * P:(c + 1) * P], ident[:, :])
                    mm.then_inc(h_turned.sem, 1)

            def logits(b):
                for n in range(width(b) // P):
                    pe.wait_ge(h_ready.sem, h_ready.at(b, bank_mates(b, n)))
                    for c in range(CC):
                        mm = nc.tensor.matmul(ps_mix[:, 0, n * EXPERTS:(n + 1) * EXPERTS],
                                              chan(b_h, b)[:, c, n * P:(n + 1) * P], gw[:, c, :],
                                              start=(c == 0), stop=(c == CC - 1))
                mm.then_inc(logits_ready.sem, 1)

            def turn_cw(b):
                pe.wait_ge(cw_ready.sem, cw_ready.at(b))
                for n in range(width(b) // P):
                    mm = nc.tensor.transpose(ps_mix[0:EXPERTS, 0, n * P:(n + 1) * P], cw[:, n, :], ident[:, :])
                mm.then_inc(cw_turned.sem, 1)

            def spread_cw(j):
                for e, _, p1 in reversed(owners(j)):
                    for n in range(width(0) // P):
                        mm = nc.tensor.matmul(ps_mix[0:p1, 1 - j, n * P:(n + 1) * P],
                                              cw[:, n, e:e + 1].to_broadcast([P, p1]), ident[:, :],
                                              start=True, stop=True)
                mm.then_inc(cw_spread.sem, 1)

            def mix(b, slot):
                if slot == 3:
                    turn_k(b)
                if slot == 14:
                    turn_x1(b)
                if slot == 17:
                    turn_h(b)
                if slot == 18:
                    logits(b)
                if slot == 20:
                    turn_cw(b)

            def by_h(b, dst, j, part):
                for c in range(CC):
                    if j == 0:
                        pe.wait_ge(h_hi_ready.sem, h_hi_ready.at(b, c + 1))
                    times_hi(dst, weights(j, part, c), h_hi[:, c, 0:width(b)], c == 0)
                for c in range(CC):
                    if j == 0:
                        pe.wait_ge(h_lo_ready.sem, h_lo_ready.at(b, c + 1))
                    mm = times_lo(dst, weights(j, part, c), h_lo[:, c, 0:width(b)], c == CC - 1)
                return mm

            def gate_up(b, j):
                n = b * TILES + j
                if first(b):
                    wait_w_lo(pe, j)
                if not (first(b) and j < 2):
                    pe.wait_ge(silu_ready.sem, n - 1)
                by_h(b, ps_gate[:, j % 2, 0:width(b)], j, 0).then_inc(gate_done.sem, 1)
                if not (first(b) and j < 2):
                    pe.wait_ge(gu_ready.sem, n - 1)
                by_h(b, ps_up[:, j % 2, 0:width(b)], j, 1).then_inc(up_done.sem, 1)

            def down(b, j):
                n = b * TILES + j
                pe.wait_ge(a_hi_ready.sem, n + 1)
                for c in range(CC):
                    if j == 0 and not first(b):
                        pe.wait_ge(out_ready.sem, out_ready.at(b - 1, c + 1))
                    times_hi(ps_y[:, c, 0:width(b)], weights(j, 2, c), a_hi[:, j % 2, 0:width(b)], j == 0)
                pe.wait_ge(a_lo_ready.sem, n + 1)
                for c in range(CC):
                    mm = times_lo(ps_y[:, c, 0:width(b)], weights(j, 2, c), a_lo[:, j % 2, 0:width(b)], j == TILES - 1)
                    if j == TILES - 1 and c == 0:
                        mm.then_inc(sum0_ready.sem, 1)
                mm.then_inc(down_done.sem, 1)

            def tiles(b, ahead):
                for j in range(1, TILES):
                    gate_up(b, j)
                    if first(b) and j == 1:
                        pe.wait_ge(cw_copied.sem, 1)
                        spread_cw(1)
                    if j >= 2:
                        down(b, j - 2)
                    if ahead:
                        mix(b + 1, j)
                down(b, TILES - 2)

            def through(b):
                tiles(b, True)
                gate_up(b + 1, 0)
                down(b, TILES - 1)

            pe.wait_ge(ident_ready.sem, 1)
            for slot in range(TILES):
                if slot == 18:
                    pe.wait_ge(params_in.sem, 64)
                if slot == 20:
                    gate_up(0, 0)
                mix(0, slot)
            spread_cw(0)
            through(0)
            with pe.Fori(1, BLOCKS - 2) as b:
                through(b)
            through(BLOCKS - 2)
            tiles(BLOCKS - 1, False)
            down(BLOCKS - 1, TILES - 1)

        @block.scalar
        def _(act):
            def load_xk(b):
                n = width(b) // STEPS
                act.dma_start(xk[:, 0:n, :], x_tok[:, bass.ds(b * (MAIN // STEPS), n), :]).then_inc(xk_in.sem, 16)

            def load_v(b):
                act.dma_start(chan(v_a, b), v_chan[:, :, bass.ds(b * MAIN, width(b))]).then_inc(v_in.sem, 16)

            def load_x(b):
                act.dma_start(chan(x_x1, b), x_chan[:, :, bass.ds(b * MAIN, width(b))]).then_inc(x_in.sem, 16)

            def split_w(j):
                act.wait_ge(w_in[j % STAGE].sem, 16 * (j // STAGE + 1))
                nc.scalar.copy(w_hi[:, j, :], w_raw[:, j % STAGE, :]).then_inc(w_hi_ready.sem, 1)

            def exps(b):
                act.wait_ge(k_turned.sem, k_turned.at(b))
                for c in range(CC):
                    last = nc.scalar.activation(chan(e1_h, b)[:, c, :], ps_mix[:, c, 0:width(b)], ACT.Exp,
                                                bias=minus_u[:, c:c + 1])
                last.then_inc(e1_ready.sem, 1)
                if not first(b):
                    act.wait_ge(cw_stored.sem, cw_stored.at(b - 1))
                for c in range(CC):
                    last = nc.scalar.activation(chan(e2_den, b)[:, c, :], ps_mix[:, c, 0:width(b)], ACT.Exp,
                                                bias=u_min[:, c:c + 1])
                last.then_inc(e2_ready.sem, 1)

            def mix(b, slot):
                if slot == 0:
                    if not first(b):
                        act.wait_ge(x1_new.sem, x1_new.at(b - 1))
                    load_xk(b)
                    load_v(b)
                if slot == 3:
                    exps(b)
                if slot == 17:
                    for i0 in range(0, width(b) // STEPS, 2):
                        i1 = bank_mates(b, i0)
                        act.wait_ge(h_turned.sem, h_turned.at(b, i1))
                        nc.scalar.copy(chan(b_h, b).rearrange("p c (n t) -> p c n t", t=STEPS)[:, :, i0:i1, :],
                                       ps_tok[:, i0:i1, :].rearrange("p n (c t) -> p c n t", c=CC)
                                       ).then_inc(h_ready.sem, i1 - i0)
                if slot == 18:
                    n = width(b) // STEPS
                    act.wait_ge(lsub_ready.sem, lsub_ready.at(b))
                    nc.scalar.activation(ex[:, 0:n, 0:EXPERTS], lsub[:, 0:n, :], ACT.Exp).then_inc(ex_ready.sem, 1)
                if slot == 20:
                    act.wait_ge(cw_turned.sem, cw_turned.at(b))
                    nc.scalar.copy(e2_den[0:EXPERTS, 0:width(b)],
                                   ps_mix[0:EXPERTS, 0, 0:width(b)]).then_inc(cw_copied.sem, 1)

            def split_h(b):
                if not first(b):
                    act.wait_ge(up_done.sem, up_done.at(b - 1))
                act.wait_ge(h_ready.sem, h_ready.at(b))
                for c in range(CC):
                    nc.scalar.copy(h_hi[:, c, 0:width(b)], chan(b_h, b)[:, c, :]).then_inc(h_hi_ready.sem, 1)

            def keep_x1(b):
                if not first(b):
                    act.wait_ge(stored.sem, stored.at(b - 1))
                act.wait_ge(x1_turned.sem, x1_turned.at(b))
                nc.scalar.copy(flat(x1, b), flat(x_x1, b)).then_inc(x1_kept.sem, 1)

            def silu(b, j):
                n = b * TILES + j
                act.wait_ge(gate_done.sem, n + 1)
                if not (first(b) and j < 2):
                    act.wait_ge(a_lo_ready.sem, n - 1)
                nc.scalar.activation(a32[:, j % 2, 0:width(b)], ps_gate[:, j % 2, 0:width(b)],
                                     ACT.Silu).then_inc(silu_ready.sem, 1)

            def round_a(b, j):
                n = b * TILES + j
                if first(b) and j + EARLY < TILES:
                    split_w(j + EARLY)
                if j == TILES - 1 and not (isinstance(b, int) and b == BLOCKS - 1):
                    split_h(b + 1)
                act.wait_ge(act_ready.sem, n + 1)
                if not (first(b) and j < 2):
                    act.wait_ge(down_done.sem, n - 1)
                nc.scalar.copy(a_hi[:, j % 2, 0:width(b)], a32[:, j % 2, 0:width(b)]).then_inc(a_hi_ready.sem, 1)

            def tile(b, j):
                silu(b, j)
                round_a(b, j)

            def tiles(b, ahead):
                if ahead and not first(b):
                    mix(b + 1, 0)
                for j in range(1, TILES):
                    if not (ahead and j - 1 in EXP_SLOTS):
                        silu(b, j)
                    round_a(b, j)
                    if ahead and j in EXP_SLOTS:
                        silu(b, j + 1)
                    if ahead:
                        mix(b + 1, j)
                    if j == 5:
                        keep_x1(b)
                        if ahead:
                            act.wait_ge(x1_kept.sem, x1_kept.at(b))
                            load_x(b + 1)

            def through(b):
                tiles(b, True)
                tile(b + 1, 0)

            mix(0, 0)
            load_x(0)
            act.wait_ge(params_in.sem, 64)
            nc.scalar.activation(g_tanh[:, :], g_raw[:, :], ACT.Tanh).then_inc(act_const.sem, 1)
            nc.scalar.activation(decay_col[:, 0, :], params[:, 0, :], ACT.Exp).then_inc(decay_exp.sem, 1)
            act.wait_ge(decay_exp.sem, 1)
            nc.scalar.activation(decay_col[:, 1, :], decay_col[:, 0, :], ACT.Exp, scale=-1.0).then_inc(act_const.sem, 1)
            act.wait_ge(u_ready.sem, 2)
            early = {2: range(0, 1), 3: range(1, 6), 17: range(6, 8), 18: range(8, EARLY)}
            for slot in range(2, TILES):
                if slot == 20:
                    silu(0, 0)
                mix(0, slot)
                if slot == 17:
                    split_h(0)
                    mix(1, 0)
                for j in early.get(slot, ()):
                    split_w(j)
            round_a(0, 0)
            through(0)
            with act.Fori(1, BLOCKS - 2) as b:
                through(b)
            through(BLOCKS - 2)
            tiles(BLOCKS - 1, False)

        @block.gpsimd
        def _(pool):
            def split_w(j):
                pool.wait_ge(w_hi_ready.sem, j + 1)
                nc.gpsimd.tensor_tensor(w_lo[:, j, :], w_raw[:, j % STAGE, :], w_hi[:, j, :].bitcast(F32),
                                        ALU.subtract).then_inc(w_lo_pool.sem, 1)

            def inverse_deviation(b, eps_done, rs_done):
                n = width(b) // STEPS
                pool.wait_ge(eps_done.sem, eps_done.at(b))
                nc.gpsimd.tensor_tensor(rs[:, 0:n], var_eps[:, 0:n], minus_half[:, 0:n],
                                        ALU.pow).then_inc(rs_done.sem, 1)

            def weigh_v_new(b):
                pool.wait_ge(v_in.sem, v_in.at(b))
                pool.wait_ge(e2_ready.sem, e2_ready.at(b))
                if not first(b):
                    pool.wait_ge(x1_new.sem, x1_new.at(b - 1))
                nc.gpsimd.tensor_tensor(flat(num_y, b), flat(e2_den, b), flat(v_a, b),
                                        ALU.mult).then_inc(ev2_ready.sem, 1)

            def weigh_v(b):
                pool.wait_ge(v_in.sem, v_in.at(b))
                pool.wait_ge(sum_b.sem, sum_b.at(b))
                nc.gpsimd.tensor_tensor(flat(e1_h, b), flat(e1_h, b), flat(v_a, b), ALU.mult).then_inc(ev_ready.sem, 1)

            def tile(b, j):
                n = b * TILES + j
                pool.wait_ge(a_hi_ready.sem, n + 1)
                nc.gpsimd.tensor_tensor(a_lo[:, j % 2, 0:width(b)], a32[:, j % 2, 0:width(b)],
                                        a_hi[:, j % 2, 0:width(b)].bitcast(F32),
                                        ALU.subtract).then_inc(a_lo_ready.sem, 1)
                if first(b) and j + EARLY < TILES and j + EARLY not in DVE_SPLITS:
                    split_w(j + EARLY)

            def tiles(b, ahead):
                for j in range(1, TILES):
                    if ahead and j == 4:
                        weigh_v_new(b + 1)
                    if ahead and j == 6:
                        weigh_v(b + 1)
                    tile(b, j)
                    if ahead and j == 1:
                        inverse_deviation(b + 1, k_eps, k_rs)
                    if ahead and j == 15:
                        inverse_deviation(b + 1, h_eps, h_rs)

            def through(b):
                tiles(b, True)
                tile(b + 1, 0)

            n0 = width(0) // STEPS
            nc.gpsimd.memset(ident[:, :], 0.0).then_inc(ident_zero.sem, 1)
            pool.wait_ge(ident_zero.sem, 1)
            nc.gpsimd.affine_select(out=ident[:, :], in_=ident[:, :], compare_op=ALU.not_equal, fill=1.0, base=0,
                                    pattern=[[-1, P]], channel_multiplier=1).then_inc(ident_ready.sem, 1)
            nc.gpsimd.memset(minus_half[:, :], -0.5).then_inc(half_ready.sem, 1)
            pool.wait_ge(half_ready.sem, 1)
            inverse_deviation(0, k_eps, k_rs)
            split_w(0)
            weigh_v_new(0)
            weigh_v(0)
            numerator(pool, 0)
            for i in range(n0 - 1):
                quotient(pool, 0, i)
            for j in range(1, EARLY_LN):
                split_w(j)
            inverse_deviation(0, h_eps, h_rs)
            for j in range(EARLY_LN, EARLY):
                split_w(j)
            tile(0, 0)
            through(0)
            with pool.Fori(1, BLOCKS - 2) as b:
                through(b)
            through(BLOCKS - 2)
            tiles(BLOCKS - 1, False)

        @block.vector
        def _(dve):
            def statistics(b, src, arrived, bn_done, mv_done, eps_done):
                n = width(b) // STEPS
                for i in range(n):
                    dve.wait_ge(arrived.sem, arrived.at(b, bank_mates(b, i)) if arrived is x1_turned else arrived.at(b))
                    last = nc.vector.bn_stats(bn[:, i, :], src[:, i, :])
                last.then_inc(bn_done.sem, 1)
                dve.wait_ge(bn_done.sem, bn_done.at(b))
                nc.vector.memset(carrier[:, :], 0.0)
                for i in range(n):
                    last = nc.vector.bn_aggr(mv[:, i, :], bn[:, i, :])
                last.then_inc(mv_done.sem, 1)
                dve.wait_ge(mv_done.sem, mv_done.at(b))
                nc.vector.tensor_scalar(var_eps[:, 0:n], mv[:, 0:n, 1], EPS, None, ALU.add).then_inc(eps_done.sem, 1)

            def normalise(b, dst, src, rs_done, norm_done):
                n = width(b) // STEPS
                dve.wait_ge(rs_done.sem, rs_done.at(b))
                for i in range(n):
                    nc.vector.tensor_scalar(dst[:, i, :], src[:, i, :], mv[:, i, 0:1], rs[:, i:i + 1],
                                            ALU.subtract, ALU.mult).then_inc(norm_done.sem, 1)

            def decayed_sums(b, dst, src, done):
                nc.vector.tensor_tensor_scan(flat(dst, b), decay[:, TOK - width(b):TOK + width(b)], flat(src, b),
                                             0.0, ALU.mult, ALU.add).then_inc(done.sem, 1)

            def route(b):
                n = width(b) // STEPS
                dve.wait_ge(ex_ready.sem, ex_ready.at(b))
                nc.vector.tensor_reduce(esum[:, 0:n], ex[:, 0:n, 0:EXPERTS], AX.X, ALU.add).then_inc(esum_ready.sem, 1)
                for i in range(n):
                    last = nc.vector.max(top[:, i, :], ex[:, i, :])
                last.then_inc(top_ready.sem, 1)
                dve.wait_ge(top_ready.sem, top_ready.at(b))
                nc.vector.memset(top[:, 0:n, TOPK:8], -1.0).then_inc(top_cut.sem, 1)
                dve.wait_ge(top_cut.sem, top_cut.at(b))
                dve.wait_ge(esum_ready.sem, esum_ready.at(b))
                nc.vector.reciprocal(rsum[:, 0:n], esum[:, 0:n]).then_inc(rsum_ready.sem, 1)
                for i in range(n):
                    last = nc.vector.match_replace(rest[:, i, :], top[:, i, :], ex[:, i, :], 0.0)
                last.then_inc(rest_ready.sem, 1)
                dve.wait_ge(rest_ready.sem, rest_ready.at(b))
                nc.vector.tensor_tensor(cw[:, 0:n, :], ex[:, 0:n, 0:EXPERTS], rest[:, 0:n, 0:EXPERTS],
                                        ALU.subtract).then_inc(cw_raw.sem, 1)
                dve.wait_ge(cw_raw.sem, cw_raw.at(b))
                dve.wait_ge(rsum_ready.sem, rsum_ready.at(b))
                nc.vector.tensor_tensor(cw[:, 0:n, :], cw[:, 0:n, :],
                                        rsum[:, 0:n].unsqueeze(2).to_broadcast([P, n, EXPERTS]),
                                        ALU.mult).then_inc(cw_ready.sem, 1)

            def new_sums(b):
                dve.wait_ge(e1_ready.sem, e1_ready.at(b))
                decayed_sums(b, b_h, e1_h, sum_b)

            def denominator(b):
                dve.wait_ge(sum_b.sem, sum_b.at(b))
                dve.wait_ge(e2_ready.sem, e2_ready.at(b))
                if not first(b):
                    dve.wait_ge(ev2_ready.sem, ev2_ready.at(b))
                add_sums(dve, b, den(b), e2_den, b_h, den_ready)

            def invert(b, piece):
                i, c = piece // CC, piece % CC
                dve.wait_ge(den_ready.sem, den_ready.at(b))
                part = chan(den(b), b)[:, c, i * STEPS + 1:(i + 1) * STEPS]
                ins = nc.vector.reciprocal(part, part)
                if c == CC - 1:
                    ins.then_inc(rden_ready.sem, 1)

            def weighed_sums(b):
                dve.wait_ge(ev_ready.sem, ev_ready.at(b))
                dve.wait_ge(v0_kept.sem, v0_kept.at(b))
                dve.wait_ge(ev2_ready.sem, ev2_ready.at(b))
                decayed_sums(b, v_a, e1_h, sum_a)

            def new_x1(b, i):
                every = slice(i * STEPS, (i + 1) * STEPS)
                dve.wait_ge(y_ready.sem, y_ready.at(b, i + 1))
                dve.wait_ge(y0_ready.sem, y0_ready.at(b))
                dve.wait_ge(x_in.sem, x_in.at(b))
                nc.vector.scalar_tensor_tensor(chan(x_x1, b)[:, :, every], chan(num_y, b)[:, :, every], g_tanh[:, 0:1],
                                               chan(x_x1, b)[:, :, every], ALU.mult, ALU.add).then_inc(x1_new.sem, 1)

            def first_steps(b):
                n = width(b) // STEPS
                dve.wait_ge(v0_kept.sem, v0_kept.at(b))
                dve.wait_ge(ev2_ready.sem, ev2_ready.at(b))
                nc.vector.tensor_copy(seqs(num_y, b)[:, :, 0], v0[:, 0:CC * n]).then_inc(y0_ready.sem, 1)

            def mix(b, slot):
                n = width(b) // STEPS
                if slot == 1:
                    statistics(b, xk, xk_in, k_bn, k_mv, k_eps)
                if slot == 2:
                    normalise(b, xk, xk, k_rs, k_norm)
                if slot == 4:
                    dve.wait_ge(v_in.sem, v_in.at(b))
                    nc.vector.tensor_copy(v0[:, 0:CC * n], seqs(v_a, b)[:, :, 0]).then_inc(v0_kept.sem, 1)
                    new_sums(b)
                if slot == 6:
                    denominator(b)
                if 7 <= slot < 7 + RECIPS:
                    for piece in range(CC * n * (slot - 7) // RECIPS, CC * n * (slot - 6) // RECIPS):
                        invert(b, piece)
                if slot == 8:
                    weighed_sums(b)
                if slot == 10:
                    numerator(dve, b)
                if slot == 11:
                    first_steps(b)
                if slot in (11, 12):
                    quotient(dve, b, slot - 11)
                    new_x1(b, slot - 11)
                if slot == 13:
                    for i in range(2, n):
                        quotient(dve, b, i)
                        new_x1(b, i)
                if slot == 15:
                    statistics(b, ps_tok, x1_turned, h_bn, h_mv, h_eps)
                if slot == 16:
                    normalise(b, tokm(e1_h, b), ps_tok, h_rs, h_norm)
                if slot == 18:
                    dve.wait_ge(logits_ready.sem, logits_ready.at(b))
                    rows = ps_mix[:, 0, 0:n * EXPERTS].rearrange("p (n e) -> p n e", n=n)
                    nc.vector.tensor_reduce(lmax[:, 0:n], rows, AX.X, ALU.max).then_inc(lmax_ready.sem, 1)
                    dve.wait_ge(lmax_ready.sem, lmax_ready.at(b))
                    nc.vector.tensor_tensor(lsub[:, 0:n, :], rows,
                                            lmax[:, 0:n].unsqueeze(2).to_broadcast([P, n, EXPERTS]),
                                            ALU.subtract).then_inc(lsub_ready.sem, 1)
                if slot == 19:
                    route(b)

            def split_h(b):
                for c in range(CC):
                    dve.wait_ge(h_hi_ready.sem, h_hi_ready.at(b, c + 1))
                    nc.vector.tensor_tensor(h_lo[:, c, 0:width(b)], chan(b_h, b)[:, c, :],
                                            h_hi[:, c, 0:width(b)].bitcast(F32),
                                            ALU.subtract).then_inc(h_lo_ready.sem, 1)

            def result(b):
                dve.wait_ge(x1_kept.sem, x1_kept.at(b))
                for c in range(CC):
                    if c == 0:
                        dve.wait_ge(sum0_ready.sem, sum0_ready.at(b))
                    else:
                        dve.wait_ge(down_done.sem, down_done.at(b))
                    nc.vector.scalar_tensor_tensor(chan(x1, b)[:, c, :], ps_y[:, c, 0:width(b)], g_tanh[:, 1:2],
                                                   chan(x1, b)[:, c, :], ALU.mult, ALU.add).then_inc(out_ready.sem, 1)

            def tile(b, j):
                n = b * TILES + j
                a = a32[:, j % 2, 0:width(b)]
                dve.wait_ge(silu_ready.sem, n + 1)
                dve.wait_ge(up_done.sem, n + 1)
                nc.vector.tensor_tensor(a, a, ps_up[:, j % 2, 0:width(b)], ALU.mult).then_inc(gu_ready.sem, 1)
                dve.wait_ge(gu_ready.sem, n + 1)
                if first(b) and j < 2:
                    dve.wait_ge(cw_spread.sem, j + 1)
                    nc.vector.tensor_tensor(a, a, ps_mix[:, 1 - j, 0:width(b)], ALU.mult).then_inc(act_ready.sem, 1)
                else:
                    dve.wait_ge(cw_in[j % 2].sem, cw_arrived(b, j))
                    nc.vector.tensor_tensor(a, a, cw_b[:, j % 2, 0:width(b)], ALU.mult).then_inc(act_ready.sem, 1)

                if first(b) and j + EARLY in DVE_SPLITS:
                    w = j + EARLY
                    dve.wait_ge(w_hi_ready.sem, w + 1)
                    nc.vector.tensor_tensor(w_lo[:, w, :], w_raw[:, w % STAGE, :], w_hi[:, w, :].bitcast(F32),
                                            ALU.subtract).then_inc(w_lo_dve.sem, 1)

            def tiles(b, ahead):
                for j in range(1, TILES):
                    tile(b, j)
                    if ahead:
                        mix(b + 1, j)
                if ahead:
                    split_h(b + 1)

            def through(b):
                tiles(b, True)
                tile(b + 1, 0)
                result(b)

            n0 = width(0) // STEPS
            nc.vector.memset(decay[:, :], 0.0).then_inc(dve_const.sem, 1)
            nc.vector.memset(ex[:, :, EXPERTS:PAD], -1.0).then_inc(dve_const.sem, 1)
            mix(0, 1)
            dve.wait_ge(params_in.sem, 64)
            nc.vector.tensor_scalar(u_min[:, :], params[:, 1, :], 0.0, None, ALU.min).then_inc(u_ready.sem, 1)
            nc.vector.tensor_scalar(minus_u[:, :], params[:, 1, :], -1.0, 0.0, ALU.mult,
                                    ALU.min).then_inc(u_ready.sem, 1)
            mix(0, 2)
            dve.wait_ge(act_const.sem, 2)
            dve.wait_ge(dve_const.sem, 2)
            for c in range(CC):
                part = decay[:, c * TOK:(c + 1) * TOK].rearrange("p (s t) -> p s t", t=STEPS)[:, :, 1:STEPS]
                nc.vector.tensor_scalar(part, part, decay_col[:, 1, c:c + 1], None, ALU.add).then_inc(dve_const.sem, 1)
            dve.wait_ge(dve_const.sem, 2 + CC)
            dve.wait_ge(v_in.sem, 16)
            nc.vector.tensor_copy(v0[:, 0:CC * n0], seqs(v_a, 0)[:, :, 0]).then_inc(v0_kept.sem, 1)
            new_sums(0)
            denominator(0)
            for piece in range(CC * n0):
                if piece == 3:
                    weighed_sums(0)
                    first_steps(0)
                invert(0, piece)
            for i in range(n0 - 1):
                new_x1(0, i)
            quotient(dve, 0, n0 - 1)
            new_x1(0, n0 - 1)
            for slot in range(14, TILES):
                mix(0, slot)
                if slot == 17:
                    split_h(0)
            tile(0, 0)
            through(0)
            with dve.Fori(1, BLOCKS - 2) as b:
                through(b)
            through(BLOCKS - 2)
            tiles(BLOCKS - 1, False)
            result(BLOCKS - 1)


def kernel(x, ctx_2048, g_xattn, g_ffn, L0_xattn_time_decay, L0_xattn_time_first,
           L0_ffn_gate_w, L0_ffn_w_gate, L0_ffn_w_up, L0_ffn_w_down):
    import numpy as np
    import concourse.bacc as bacc
    from concourse.bass_utils import run_bass_kernel_spmd

    def chan_major(a):
        return np.ascontiguousarray(np.asarray(a).reshape(TOKENS, CC, P).transpose(2, 1, 0))

    def row_tiles(a):
        return a.reshape(TILES, P, CC, P).transpose(0, 3, 2, 1).reshape(TILES, P, CH)

    w_gate, w_up, w_down = np.asarray(L0_ffn_w_gate), np.asarray(L0_ffn_w_up), np.asarray(L0_ffn_w_down)
    arrays = {
        "x_tok": np.ascontiguousarray(np.asarray(x).transpose(1, 0, 2)),
        "x_chan": chan_major(x),
        "v_chan": chan_major(ctx_2048),
        "w_all": np.ascontiguousarray(np.concatenate(
            [row_tiles(w_gate), row_tiles(w_up), w_down.transpose(0, 2, 1).reshape(TILES, P, CH)], axis=2)),
        "gate_w": np.ascontiguousarray(np.asarray(L0_ffn_gate_w).reshape(EXPERTS, CC, P).transpose(2, 1, 0)),
        "decay_u": np.ascontiguousarray(np.stack(
            [np.asarray(L0_xattn_time_decay), np.asarray(L0_xattn_time_first)]).reshape(2, CC, P).transpose(2, 0, 1)),
        "gates": np.concatenate([np.asarray(g_xattn), np.asarray(g_ffn)]),
    }
    nc = bacc.Bacc("TRN2", target_bir_lowering=False, num_devices=1)
    args = [nc.dram_tensor(name, a.shape, mybir.dt.from_np(a.dtype), kind="ExternalInput").ap()
            for name, a in arrays.items()]
    out = nc.dram_tensor("out", (P, CC, TOKENS), F32, kind="ExternalOutput").ap()
    program(nc, *args, out)
    r = run_bass_kernel_spmd(nc, [arrays], core_ids=[0])
    return np.ascontiguousarray(r.results[0]["out"].transpose(2, 1, 0)).reshape(SEQS, STEPS, CH)
```
